# Optimizing a Trainium2 kernel written in Bass

```python
import numpy as np
import jax
import jax.numpy as jnp

def _softmax(x, axis=-1):
    return jax.nn.softmax(x, axis=axis)

def _gelu(x):
    return jax.nn.gelu(x, approximate=True)

def _silu(x):
    return jax.nn.silu(x)

def _sigmoid(x):
    return jax.nn.sigmoid(x)

def _layernorm(x, axis=-1, eps=1e-05):
    m = jnp.mean(x, axis=axis, keepdims=True)
    v = jnp.var(x, axis=axis, keepdims=True)
    return (x - m) / jnp.sqrt(v + eps)

def _scatter_add(tgt, idx, src, axis=0):
    return tgt.at[idx].add(src)

def _segment_sum(src, seg, n):
    return jax.ops.segment_sum(src, seg, n)
kernel_name = 'mk_gnn_resnorm_d1_gnn_r8_fbd0d4'

def setup_inputs(seed: int=0):
    np.random.seed(seed)
    _w = jnp.asarray

    def _rec_inputs():
        import jax
        import jax.numpy as jnp
        _gk = jax.random.key(seed)
        x = -0.0002117 + 1 * jax.random.normal(jax.random.fold_in(_gk, 1), (1250, 1024), jnp.float32)
        src = jax.random.randint(jax.random.fold_in(_gk, 2), (40000,), 0, 1250, jnp.int32)
        dst = jnp.minimum((1250 * jax.random.uniform(jax.random.fold_in(_gk, 3), (40000,)) ** 2.0).astype(jnp.int32), 9999)
        _o = jnp.argsort(dst, stable=True)
        src = src[_o]
        dst = dst[_o]
        return (x, src, dst)
    x, src, dst = _rec_inputs()

    def _L0_gnn_setup():
        import jax, jax.numpy as jnp
        import numpy as np
        N_NODES = 3125
        N_EDGES = 50000
        D = 1024

        def _sage_layer(h, edge_src, edge_dst, deg_inv, W_self, W_neigh, b):
            msg = h[edge_src]
            agg = jax.ops.segment_sum(msg, edge_dst, num_segments=h.shape[0])
            mean = agg * deg_inv[:, None]
            return h @ W_self + mean @ W_neigh + b
        key = jax.random.key(seed)
        ks = jax.random.split(key, 8)
        s = 1.0 / np.sqrt(D)
        return {'x': jax.random.normal(ks[0], (N_NODES, D), dtype=jnp.float32), 'edge_src': jax.random.randint(ks[1], (N_EDGES,), 0, N_NODES, dtype=jnp.int32), 'edge_dst': jax.random.randint(ks[2], (N_EDGES,), 0, N_NODES, dtype=jnp.int32), 'W_self0': jax.random.normal(ks[3], (D, D), dtype=jnp.float32) * s, 'W_neigh0': jax.random.normal(ks[4], (D, D), dtype=jnp.float32) * s, 'b0': jnp.zeros((D,), dtype=jnp.float32), 'W_self1': jax.random.normal(ks[5], (D, D), dtype=jnp.float32) * s, 'W_neigh1': jax.random.normal(ks[6], (D, D), dtype=jnp.float32) * s, 'b1': jnp.zeros((D,), dtype=jnp.float32)}
    _L0_gnn_all = _L0_gnn_setup()
    _L0_gnn_in = {k: v for k, v in _L0_gnn_all.items() if k in ('W_self0', 'W_neigh0', 'b0', 'W_self1', 'W_neigh1', 'b1')}
    del _L0_gnn_all
    return {'x': x, 'src': src, 'dst': dst, 'L0_gnn_W_self0': _L0_gnn_in['W_self0'], 'L0_gnn_W_neigh0': _L0_gnn_in['W_neigh0'], 'L0_gnn_b0': _L0_gnn_in['b0'], 'L0_gnn_W_self1': _L0_gnn_in['W_self1'], 'L0_gnn_W_neigh1': _L0_gnn_in['W_neigh1'], 'L0_gnn_b1': _L0_gnn_in['b1']}

def reference(x, src, dst, L0_gnn_W_self0, L0_gnn_W_neigh0, L0_gnn_b0, L0_gnn_W_self1, L0_gnn_W_neigh1, L0_gnn_b1):
    import jax
    import jax.numpy as jnp

    def _L0_gnn_ref(x, edge_src, edge_dst, W_self0, W_neigh0, b0, W_self1, W_neigh1, b1):
        import jax, jax.numpy as jnp
        import numpy as np
        N_NODES = 3125
        N_EDGES = 50000
        D = 1024

        def _sage_layer(h, edge_src, edge_dst, deg_inv, W_self, W_neigh, b):
            msg = h[edge_src]
            agg = jax.ops.segment_sum(msg, edge_dst, num_segments=h.shape[0])
            mean = agg * deg_inv[:, None]
            return h @ W_self + mean @ W_neigh + b
        N = x.shape[0]
        deg = jax.ops.segment_sum(jnp.ones_like(edge_dst, dtype=x.dtype), edge_dst, num_segments=N)
        deg_inv = 1.0 / jnp.maximum(deg, 1.0)
        h = jax.nn.relu(_sage_layer(x, edge_src, edge_dst, deg_inv, W_self0, W_neigh0, b0))
        out = _sage_layer(h, edge_src, edge_dst, deg_inv, W_self1, W_neigh1, b1)
        return out
    x = _layernorm(x + _L0_gnn_ref(x, src, dst, L0_gnn_W_self0, L0_gnn_W_neigh0, L0_gnn_b0, L0_gnn_W_self1, L0_gnn_W_neigh1, L0_gnn_b1), axis=-1)
    return x

_drawn_inputs = setup_inputs


def setup_inputs(seed=0):
    import zlib

    import numpy as np

    out = dict(_drawn_inputs(seed))
    spreads = {'L0_gnn_b0': (0.0, 0.1), 'L0_gnn_b1': (0.0, 0.1)}
    factors = {}
    for name, (base, spread) in spreads.items():
        noise = np.random.default_rng([zlib.crc32(name.encode()), seed]).standard_normal(out[name].shape)
        drawn = base * np.exp(spread * noise) if base else spread * noise
        out[name] = jnp.asarray(drawn.astype(out[name].dtype))
    for name, factor in factors.items():
        out[name] = (out[name] * factor).astype(out[name].dtype)
    return out
```

```python
from contextlib import ExitStack

import concourse.bass as bass
from concourse import mybir

ALU = mybir.AluOpType
ACT = mybir.ActivationFunctionType
AX = mybir.AxisListType
F32 = mybir.dt.float32
F16 = mybir.dt.float16
I32 = mybir.dt.int32
U16 = mybir.dt.uint16
RMAX = bass.bass_isa.ReduceOp.max

P = 128
WIN = 40
CK = 4
ZK = 2 * P


def gnn_kernel(nc, x, src, dst, Wn0, Ws0, b0, Wn1, Ws1, b1, out):
    N, D = x.shape
    E = src.shape[0]
    TP = 125
    JT = N // TP
    KT = D // P
    HD = D // 2
    GE = CK * TP
    NG = E // GE
    NWIN = -(-N // WIN)
    NPAD = NWIN * WIN
    HN = JT * WIN
    assert N == TP * JT and D == P * KT and E == GE * NG and HD <= 512 and HN <= 512
    CH = [420, 420, N - 840]
    CO = [0, 420, 840]
    BLK = JT * P
    EARLY = 10
    PAIRS = NG // 2
    GT = 6
    IT = JT // 2
    assert EARLY * 2 + GT * JT == NG

    with ExitStack() as ctx:
        def sb(name, shape, dt):
            return ctx.enter_context(nc.sbuf_tensor(name, shape, dt))

        def sem(name):
            return ctx.enter_context(nc.semaphore(name))

        xz = sb("xz", [P, 2 * JT * D], F16)
        zh = sb("zh", [P, KT + 1, 2, BLK], F16)
        wn = sb("wn", [P, KT + 1, 2, D], F16)
        ws = sb("ws", [P, KT + 1, 2, D], F16)
        A = sb("A", [P, JT, NPAD], U16)
        scratch = sb("scratch", [P, 5120], F16)
        lohot = sb("lohot", [P, 2, CK, P], F16)
        table = sb("table", [P, 5, CK, NG], F32)
        basebc = sb("basebc", [P, NG], F32)
        base_i = sb("base_i", [1, NG], I32)
        iota_lo = sb("iota_lo", [P, TP + 3], F16)
        iota_q = sb("iota_q", [P, HN], F16)
        ident = sb("ident", [P, P], F32)
        ones = sb("ones", [P, P], F32)
        ones16 = sb("ones16", [P, P], F16)
        dinvT = sb("dinvT", [P, JT], F32)
        b0c = sb("b0c", [P, KT], F32)
        b0h = sb("b0h", [P, KT], F32)
        mx = sb("mx", [P, 5 * KT + 16], F32)
        hmx = sb("hmx", [P, 3 * KT], F32)
        S = sb("S", [P, 64], F32)
        nwin_i = sb("nwin_i", [1, 2], I32)
        st = sb("st", [P, 2, 12], F32)
        mv = sb("mv", [P, 2, 2], F32)
        ln = sb("ln", [P, 2, 4], F32)
        ps = ctx.enter_context(nc.psum_tensor("ps", [P, 8, 512], F32))

        xT = [xz[:, i * KT * N:(i + 1) * KT * N].rearrange("p (k n) -> p k n", k=KT) for i in range(2)]
        z1 = [xz[0:TP, i * JT * D:(i + 1) * JT * D].rearrange("p (j d) -> p j d", j=JT) for i in range(2)]
        zflat = zh[:].rearrange("p k h n -> p (k h n)")
        xraw = zflat[:, 0:2 * JT * D].bitcast(F32).rearrange("p (j d) -> p j d", j=JT)
        lo, q, hi, dcol, inside = (table[:, i] for i in range(5))
        dinvbc = table[:].rearrange("p a k g -> p (a k g)")[:, 0:N]
        AF = A[:].bitcast(F16)
        A32 = A[:].bitcast(I32)
        qhot = scratch[:, 0:2 * CK * HN].rearrange("p (s c n) -> p s c n", s=2, c=CK)
        stage = scratch[:, 2 * CK * HN:2 * CK * HN + 2 * HN].bitcast(U16).rearrange("p (s j w) -> p s j w", s=2, j=JT)
        stage32 = scratch[:, 2 * CK * HN:2 * CK * HN + 2 * HN].bitcast(I32).rearrange("p (s j w) -> p s j w", s=2, j=JT)
        pre = scratch[:, 0:2 * 3 * 420].bitcast(F32).rearrange("p (n c) -> p n c", n=3)
        h32 = scratch[:, 2 * 3 * 420:4 * 3 * 420].bitcast(F32).rearrange("p (n c) -> p n c", n=3)
        dprod = scratch[:, 0:2 * N].bitcast(F32)
        eraw = xz[0:NG, 0:4 * GE].bitcast(I32).rearrange("p (t e) -> p t e", t=2)
        ef = xz[0:NG, 4 * GE:8 * GE].bitcast(F32).rearrange("p (t e) -> p t e", t=2)
        eb = xz[0:NG, 8 * GE:8 * GE + 2 * NG + 4].bitcast(F32)
        wnf = wn[:].rearrange("p k h d -> p k (h d)").bitcast(F32)
        b1bc = wnf[0:TP, 0, :]
        xres = [wnf[0:TP, 1 + i, :] for i in range(2)]
        ybuf = [wnf[0:TP, 3 + i, :] for i in range(2)]
        obuf = [wnf[0:TP, 5 + i, :] for i in range(2)]

        def raw(w, k, n=1):
            return w[:, k + 1:k + 1 + n].rearrange("p k h d -> p k (h d)").bitcast(F32)

        def bank(b, n=2):
            return ps[:, b:b + n, :].rearrange("p b c -> p (b c)")

        col = {}

        def c(name, rows=P):
            i = col.setdefault(name, len(col))
            assert i < 64
            return S[0:rows, i:i + 1]

        edges_in = sem("edges_in")
        x_in = [sem(f"x_in{j}") for j in range(JT)]
        wn0_in = [sem(f"wn0_in{k}") for k in range(KT // 2)]
        w_in = {n: sem(f"{n}_in") for n in ("ws0", "wn1", "ws1")}
        b0_in = sem("b0_in")
        b1_in = sem("b1_in")
        consts_ready = sem("consts_ready")
        A_zeroed = sem("A_zeroed")
        dve_step = sem("dve_step")
        pool_step = sem("pool_step")
        edges_float = sem("edges_float")
        edges_turned = sem("edges_turned")
        edges_diag = sem("edges_diag")
        edges_spread = sem("edges_spread")
        table_ready = sem("table_ready")
        onehots_made = sem("onehots_made")
        counts_ready = sem("counts_ready")
        counts_copied = sem("counts_copied")
        counts_added = sem("counts_added")
        passed = sem("passed")
        win_step = sem("win_step")
        max_done = sem("max_done")
        maxes_ready = sem("maxes_ready")
        max_spread = sem("max_spread")
        scale_ready = sem("scale_ready")
        panel_ready = sem("panel_ready")
        high_ready = sem("high_ready")
        panel_out = sem("panel_out")
        w_high = sem("w_high")
        w_low = sem("w_low")
        A_ready = sem("A_ready")
        deg_ready = sem("deg_ready")
        dinv_ready = sem("dinv_ready")
        unit_ready = sem("unit_ready")
        pre_ready = sem("pre_ready")
        dsum = sem("dsum")
        h32_ready = sem("h32_ready")
        h_high = sem("h_high")
        h_low = sem("h_low")
        out_ready = sem("out_ready")
        x_again = [sem(f"x_again{i}") for i in range(2)]
        xb_ready = sem("xb_ready")
        y_part = sem("y_part")
        y_ready = sem("y_ready")
        stat_ready = sem("stat_ready")
        aggr_ready = sem("aggr_ready")
        var_ready = sem("var_ready")
        std_ready = sem("std_ready")
        rstd_ready = sem("rstd_ready")
        shift_ready = sem("shift_ready")
        o_ready = sem("o_ready")
        o_stored = [sem(f"o_stored{i}") for i in range(2)]

        block = ctx.enter_context(nc.Block())

        WN = {"wn0": (wn, Wn0), "ws0": (ws, Ws0), "wn1": (wn, Wn1), "ws1": (ws, Ws1)}
        ORDER = ["x", "wn0", "b0", "ws0", "wn1", "h", "ws1"]
        SPLIT = ["wn0", "ws0", "wn1", "ws1"]

        def load_weights(eng, name):
            buf, dram = WN[name]
            d = dram.rearrange("(k p) d -> p k d", p=P)
            for k in range(0, KT, 2):
                landed = wn0_in[k // 2] if name == "wn0" else w_in[name]
                eng.dma_start(raw(buf, k, 2), d[:, k:k + 2, :]).then_inc(landed, 16)

        def apart(eng):
            eng.sem_inc(passed, 1)

        @block.sync
        def _(sp):
            sp.dma_start(eraw[:, 0, :], dst.rearrange("(g e) -> g e", e=GE)).then_inc(edges_in, 16)
            sp.dma_start(eraw[:, 1, :], src.rearrange("(g e) -> g e", e=GE)).then_inc(edges_in, 16)
            for j in range(JT):
                sp.dma_start(xraw[0:TP, j, :], x[j * TP:(j + 1) * TP, :]).then_inc(x_in[j], 16)
            load_weights(sp, "wn0")
            load_weights(sp, "ws0")
            sp.dma_start(b0c[:], b0.rearrange("(f p) -> p f", p=P), allow_slow_non_contiguous=True).then_inc(b0_in, 16)
            sp.wait_ge(panel_ready, 2 * JT)
            load_weights(sp, "wn1")
            sp.wait_ge(unit_ready, 3 * KT)
            load_weights(sp, "ws1")
            sp.wait_ge(panel_ready, 3 * JT)
            sp.dma_start(b1bc, b1.rearrange("(a d) -> a d", a=1).to_broadcast([TP, D])).then_inc(b1_in, 16)

            def rows(i):
                for r in range(2):
                    t = 2 * i + r
                    if not isinstance(i, int) or i >= 1:
                        sp.wait_ge(y_part, t - 1)
                    sp.dma_start(xres[r], x[bass.ds(t * TP, TP), :]).then_inc(x_again[r], 16)

            rows(0)
            with sp.Fori(1, IT) as i:
                rows(i)

        @block.gpsimd
        def _(pool):
            own = [0]

            def link(ins):
                own[0] += 1
                ins.then_inc(pool_step, 1)
                pool.wait_ge(pool_step, own[0])

            link(pool.memset(ones[:], 1.0))
            link(pool.memset(ones16[:], 1.0))
            link(pool.affine_select(out=ident[:], in_=ones[:], compare_op=ALU.is_equal, fill=0.0, base=0,
                                    pattern=[[-1, P]], channel_multiplier=1))
            link(pool.memset(mx[:], 0.0))
            pool.iota(iota_lo[:, 0:TP], [[1, TP]], base=0, channel_multiplier=0,
                      allow_small_or_imprecise_dtypes=True).then_inc(consts_ready, 1)
            pool.iota(iota_q[:], [[1, HN]], base=0, channel_multiplier=0,
                      allow_small_or_imprecise_dtypes=True).then_inc(consts_ready, 1)
            pool.memset(A[:], 0).then_inc(A_zeroed, 1)
            pool.wait_ge(A_zeroed, 1)
            pool.wait_ge(table_ready, 1)
            nwin = pool.value_load(nwin_i[0:1, 0:1], min_val=1, max_val=NWIN)

            def add(s, r, first, base=None):
                if base is None:
                    base = pool.value_load(base_i[0:1, bass.ds(s, 1)], min_val=0, max_val=(NPAD - WIN) // 2)
                if not first:
                    pool.wait_ge(counts_added, s)
                pool.wait_ge(counts_copied, s + 1)
                apart(pool)
                a = A32[0:TP, :, bass.ds(base, WIN // 2)]
                pool.tensor_tensor(a, a, stage32[0:TP, r], ALU.add).then_inc(counts_added, 1)

            def pair(i):
                for r in range(2):
                    add(2 * i + r, r, isinstance(i, int) and i == 0 and r == 0)

            def spread(n):
                pool.wait_ge(maxes_ready, n + 1)
                pool.partition_all_reduce(c("all" + ORDER[n]), c("max" + ORDER[n]), P, RMAX).then_inc(max_spread, 1)

            pair(0)
            with pool.Fori(1, EARLY) as i:
                pair(i)
            spread(0)
            spread(1)
            spread(2)
            with pool.Fori(EARLY, EARLY + 2 * GT) as i:
                pair(i)
            spread(3)
            with pool.Fori(EARLY + 2 * GT, PAIRS) as i:
                pair(i)
            with pool.If(nwin > 1):
                with pool.Fori(1, nwin) as w:
                    with pool.Fori(0, PAIRS) as i:
                        for r in range(2):
                            add(w * NG + 2 * i + r, r, False, base=w * (WIN // 2))
            for n in range(4, 7):
                spread(n)
            pool.wait_ge(b1_in, 16)

            def residual(i):
                for r in range(2):
                    pool.wait_ge(x_again[r], 16 * (i + 1))
                    pool.tensor_tensor(xres[r], xres[r], b1bc, ALU.add).then_inc(xb_ready, 1)

            with pool.Fori(0, IT) as i:
                residual(i)

        @block.tensor
        def _(pe):
            pe.wait_ge(consts_ready, 2)
            for t in range(2):
                pe.wait_ge(edges_float, t + 1)
                for k in range(CK):
                    ins = pe.transpose(ps[0:TP, 6 + t, k * NG:(k + 1) * NG], ef[:, t, k * TP:(k + 1) * TP],
                                       ident[0:NG, 0:NG])
                ins.then_inc(edges_turned, 1)
            pe.wait_ge(edges_diag, 1)
            pe.matmul(ps[:, 5, 0:NG + 2], ones[0:NG, :], eb[:, 0:NG + 2], start=True, stop=True).then_inc(
                edges_spread, 1)

            def count(s, r, first):
                pe.wait_ge(onehots_made, s + 1)
                if not first:
                    pe.wait_ge(counts_copied, s - 1)
                for k in range(CK):
                    ins = pe.matmul(ps[0:TP, 6 + r, 0:HN], lohot[0:TP, r, k, 0:TP], qhot[0:TP, r, k, :],
                                    start=(k == 0), stop=(k == CK - 1))
                ins.then_inc(counts_ready, 1)

            def pair(i):
                for r in range(2):
                    count(2 * i + r, r, isinstance(i, int) and i == 0)

            pe.wait_ge(table_ready, 1)
            nwin = pe.value_load(nwin_i[0:1, 0:1], min_val=1, max_val=NWIN)
            pair(0)
            with pe.Fori(1, EARLY) as i:
                pair(i)

            for j in range(JT):
                pe.wait_ge(x_in[j], 16)
                if j >= 2:
                    pe.wait_ge(panel_out, j - 1)
                for k in range(KT):
                    b, o = divmod(k * P, 512)
                    ins = pe.transpose(ps[:, 2 * (j % 2) + b, o:o + TP], xraw[0:TP, j, k * P:(k + 1) * P],
                                       ident[0:TP, 0:TP])
                ins.then_inc(panel_ready, 1)

            def panel(i, r, lhs, w, done, beside=None):
                t = 2 * i + r
                pe.wait_ge(panel_out, t + done - 1)
                for k in range(KT):
                    if beside and k < GT:
                        beside(t, k)
                    for a, bs in ((0, (0, 1)), (1, (0,))):
                        for b in bs:
                            for half in range(2):
                                ins = pe.matmul(ps[0:TP, 2 * r + half, :], lhs(a, k, t),
                                                w[:, k, b, half * HD:(half + 1) * HD],
                                                start=(k == 0 and a == 0 and b == 0),
                                                stop=(k == KT - 1 and a == 1))
                ins.then_inc(panel_ready, 1)

            pe.wait_ge(panel_out, JT)
            pe.wait_ge(w_low, KT)
            with pe.Fori(0, IT) as i:
                for r in range(2):
                    panel(i, r, lambda a, k, t: xT[a][:, k, bass.ds(t * TP, TP)], wn, JT,
                          beside=lambda t, k: count(2 * EARLY + t * GT + k, k % 2, False))
            with pe.If(nwin > 1):
                with pe.Fori(1, nwin) as w:
                    with pe.Fori(0, PAIRS) as i:
                        for r in range(2):
                            count(w * NG + 2 * i + r, r, False)

            pe.wait_ge(A_ready, 1)
            for n in range(3):
                for j in range(JT):
                    ins = pe.matmul(ps[:, (6, 7, 5)[n], 0:CH[n]], ones16[0:TP, :], AF[0:TP, j, CO[n]:CO[n] + CH[n]],
                                    start=(j == 0), stop=(j == JT - 1))
                ins.then_inc(deg_ready, 1)

            pe.wait_ge(w_low, 2 * KT)
            pe.wait_ge(panel_out, 2 * JT)
            pe.wait_ge(dinv_ready, 1)

            def unit(f, n):
                if not isinstance(f, int):
                    pe.wait_ge(pre_ready, 3 * f + n - 2)
                for k in range(KT):
                    for a, b in ((0, 0), (0, 1), (1, 0)):
                        pe.matmul(ps[:, 3 + n, 0:CH[n]], ws[:, k, a, bass.ds(f * P, P)],
                                  xT[b][:, k, CO[n]:CO[n] + CH[n]],
                                  start=(k == 0 and a == 0 and b == 0), stop=(k == KT - 1 and a == 1))
                for j in range(JT):
                    for a in range(2):
                        ins = pe.matmul(ps[:, n, 0:CH[n]], zflat[0:TP, bass.ds((2 * f + 2 + a) * BLK + j * P, P)],
                                        AF[0:TP, j, CO[n]:CO[n] + CH[n]],
                                        start=(j == 0 and a == 0), stop=(j == JT - 1 and a == 1))
                ins.then_inc(unit_ready, 1)

            for n in range(3):
                unit(0, n)
            with pe.Fori(1, KT) as f:
                for n in range(3):
                    unit(f, n)

            pe.wait_ge(h_low, 3 * KT)
            pe.wait_ge(w_low, 3 * KT)
            with pe.Fori(0, IT) as i:
                for r in range(2):
                    panel(i, r, lambda a, k, t: zh[:, k, a, bass.ds(t * TP, TP)], wn, 2 * JT)

            pe.wait_ge(w_low, 4 * KT)

            def tile(i, r, first):
                t = 2 * i + r
                g = 4 * (1 - r)
                if not first:
                    pe.wait_ge(y_ready, t - 1)
                elif r == 1:
                    pe.wait_ge(panel_out, 3 * JT)
                for k in range(KT):
                    for a, bs in ((0, (0, 1)), (1, (0,))):
                        for b in bs:
                            for half in range(2):
                                pe.matmul(ps[0:TP, g + half, :], zh[:, k, a, bass.ds(t * TP, TP)],
                                          ws[:, k, b, half * HD:(half + 1) * HD],
                                          start=(k == 0 and a == 0 and b == 0), stop=(k == KT - 1 and a == 1))
                if first and r == 0:
                    pe.wait_ge(panel_out, 3 * JT)
                for j in range(JT):
                    for b in range(2):
                        for half in range(2):
                            ins = pe.matmul(ps[0:TP, g + 2 + half, :], AF[0:TP, j, bass.ds(t * TP, TP)],
                                            z1[b][:, j, half * HD:(half + 1) * HD],
                                            start=(j == 0 and b == 0), stop=(j == JT - 1 and b == 1))
                ins.then_inc(out_ready, 1)

            tile(0, 0, True)
            tile(0, 1, True)
            with pe.Fori(1, IT) as i:
                for r in range(2):
                    tile(i, r, False)

        @block.scalar
        def _(act):
            def take(s, r, first):
                act.wait_ge(counts_ready, s + 1)
                if not first:
                    act.wait_ge(counts_added, s - 1)
                act.activation(stage[0:TP, r], ps[0:TP, 6 + r, 0:HN].rearrange("p (j w) -> p j w", j=JT),
                               ACT.Copy).then_inc(counts_copied, 1)

            def pair(i):
                for r in range(2):
                    take(2 * i + r, r, isinstance(i, int) and i == 0)

            act.wait_ge(table_ready, 1)
            nwin = act.value_load(nwin_i[0:1, 0:1], min_val=1, max_val=NWIN)
            pair(0)
            with act.Fori(1, EARLY) as i:
                pair(i)

            act.wait_ge(scale_ready, 1)
            for j in range(JT):
                act.wait_ge(panel_ready, j + 1)
                act.activation(xT[0][:, :, j * TP:(j + 1) * TP],
                               bank(2 * (j % 2)).rearrange("p (k n) -> p k n", n=P)[:, :, 0:TP],
                               ACT.Copy, scale=c("s_x")).then_inc(high_ready, 1)

            def split(name, k):
                n = SPLIT.index(name)
                if not isinstance(k, int) or k >= 1:
                    act.wait_ge(w_low, n * KT + k)
                w = WN[name][0]
                act.activation(w[:, bass.ds(k, 1), 0, :].rearrange("p k d -> p (k d)"),
                               w[:, bass.ds(k + 1, 1)].rearrange("p k h d -> p (k h d)").bitcast(F32),
                               ACT.Copy, scale=c("s_" + name)).then_inc(w_high, 1)

            act.wait_ge(scale_ready, 2)
            for k in range(KT):
                split("wn0", k)

            def panels(i, layer, works):
                for r in range(2):
                    t = 2 * i + r
                    works(i, r)
                    act.wait_ge(panel_ready, (1 + layer) * JT + t + 1)
                    p = bank(2 * r)[0:TP]
                    if layer == 0:
                        act.activation(z0out(0, t), p.rearrange("p (f c) -> p f c", f=KT), ACT.Copy,
                                       scale=2.0 ** -23).then_inc(high_ready, 1)
                    else:
                        act.activation(z1[0][:, bass.ds(t, 1), :].rearrange("p j d -> p (j d)"), p, ACT.Copy,
                                       scale=c("s_z1", TP)).then_inc(high_ready, 1)

            def z0out(a, t):
                return zh[0:TP, 1:KT + 1, a, bass.ds(t * P, P)]

            def beside(i, r, name=None, groups=True):
                for g in range(GT):
                    if groups:
                        take(2 * EARLY + (2 * i + r) * GT + g, g % 2, False)
                    if name and g in (1, 3):
                        split(name, 4 * i - 8 + 2 * r + g // 2)

            with act.Fori(0, 2) as i:
                panels(i, 0, beside)
            act.wait_ge(scale_ready, 3)
            with act.Fori(2, 4) as i:
                panels(i, 0, lambda i, r: beside(i, r, "ws0"))
            panels(4, 0, beside)
            with act.If(nwin > 1):
                with act.Fori(1, nwin) as w:
                    with act.Fori(0, PAIRS) as i:
                        for r in range(2):
                            take(w * NG + 2 * i + r, r, False)

            act.wait_ge(dinv_ready, 1)

            def unit(f, n):
                v = 3 * f + n
                act.wait_ge(pre_ready, v + 1)
                apart(act)
                act.activation(h32[:, n, 0:CH[n]], pre[:, n, 0:CH[n]], ACT.Relu,
                               bias=b0h[:, bass.ds(f, 1)]).then_inc(h32_ready, 1)
                act.wait_ge(h32_ready, v + 1)
                act.activation(zflat[:, bass.ds(2 * f * BLK + CO[n], CH[n])], h32[:, n, 0:CH[n]],
                               ACT.Copy).then_inc(h_high, 1)

            with act.Fori(0, KT // 2) as f:
                for n in range(3):
                    unit(f, n)
            act.wait_ge(scale_ready, 4)
            with act.Fori(KT // 2, KT) as f:
                for n in range(3):
                    unit(f, n)
                for k in range(2):
                    split("wn1", 2 * f - KT + k)

            act.wait_ge(scale_ready, 5)
            with act.Fori(0, 2) as i:
                panels(i, 1, lambda i, r: None)
            act.wait_ge(scale_ready, 6)
            with act.Fori(2, 4) as i:
                panels(i, 1, lambda i, r: beside(i, r, "ws1", groups=False))
            panels(4, 1, lambda i, r: None)

            def finish(i, r, first):
                t = 2 * i + r
                act.wait_ge(var_ready, t + 1)
                act.activation(ln[0:TP, r, 1:2], ln[0:TP, r, 0:1], ACT.Sqrt).then_inc(std_ready, 1)
                act.wait_ge(shift_ready, t + 1)
                if not first:
                    act.wait_ge(o_stored[r], 16 * i)
                act.activation(obuf[r], ybuf[r], ACT.Identity, bias=ln[0:TP, r, 3:4],
                               scale=ln[0:TP, r, 2:3]).then_inc(o_ready, 1)
                act.wait_ge(o_ready, t + 1)
                act.dma_start(out[bass.ds(t * TP, TP), :], obuf[r]).then_inc(o_stored[r], 16)

            finish(0, 0, True)
            finish(0, 1, True)
            with act.Fori(1, IT) as i:
                for r in range(2):
                    finish(i, r, False)
            for r in range(2):
                act.wait_ge(o_stored[r], 16 * IT)

        @block.vector
        def _(dve):
            own = [0]

            def link(ins):
                own[0] += 1
                ins.then_inc(dve_step, 1)
                dve.wait_ge(dve_step, own[0])

            dve.wait_ge(edges_in, 32)
            for t in range(2):
                dve.tensor_copy(ef[:, t, :], eraw[:, t, :]).then_inc(edges_float, 1)
            dve.wait_ge(edges_float, 2)
            base, top, span, one = (c(x, NG) for x in ("base", "top", "span", "same"))
            link(dve.tensor_reduce(base, ef[:, 0, :], AX.X, ALU.min))
            link(dve.tensor_reduce(top, ef[:, 0, :], AX.X, ALU.max))
            R = 1.5 * 2.0 ** 23
            link(dve.tensor_scalar(base, base, 0.5, -0.25, ALU.mult, ALU.add))
            link(dve.tensor_scalar(base, base, R, -R, ALU.add, ALU.add))
            link(dve.tensor_scalar(base, base, 2.0, float(NPAD - WIN), ALU.mult, ALU.min))
            link(dve.tensor_tensor(span, top, base, ALU.subtract))
            dve.wait_ge(consts_ready, 2)
            link(dve.tensor_scalar(eb[:, 0:NG], ident[0:NG, 0:NG], base, None, ALU.mult))
            link(dve.tensor_scalar(eb[:, NG:NG + 1], span, float(WIN), None, ALU.is_ge))
            link(dve.tensor_reduce(one, ef[:, 0, :], AX.X, ALU.min))
            dve.tensor_tensor(eb[:, NG + 1:NG + 2], top, one, ALU.is_equal).then_inc(edges_diag, 1)

            dve.wait_ge(edges_turned, 2)
            lov, hiv, dv = lo[0:TP], hi[0:TP], dcol[0:TP]
            srcp = ps[0:TP, 7, 0:CK * NG].rearrange("p (k g) -> p k g", k=CK)
            dstp = ps[0:TP, 6, 0:CK * NG].rearrange("p (k g) -> p k g", k=CK)
            link(dve.tensor_scalar(lov, srcp, 1.0 / TP, 0.5 / TP - 0.5, ALU.mult, ALU.add))
            link(dve.tensor_scalar(hiv, lov, R, -R, ALU.add, ALU.add))
            link(dve.scalar_tensor_tensor(lov, hiv, -float(TP), srcp, ALU.mult, ALU.add))
            link(dve.tensor_scalar(hiv, hiv, float(WIN), 1.0, ALU.mult, ALU.add))
            link(dve.tensor_copy(dv, dstp))
            dve.wait_ge(edges_spread, 1)
            link(dve.tensor_copy(basebc[:], ps[:, 5, 0:NG]))
            f1, f2 = c("f1", 1), c("f2", 1)
            link(dve.tensor_scalar(f1, ps[0:1, 5, NG:NG + 1], 1.0, None, ALU.is_ge))
            link(dve.tensor_scalar(f2, ps[0:1, 5, NG + 1:NG + 2], 3.0, None, ALU.is_ge))
            link(dve.tensor_tensor(f1, f1, f2, ALU.max))
            link(dve.tensor_scalar(f2, f1, float(NWIN - 1), 1.0, ALU.mult, ALU.add))
            link(dve.tensor_copy(nwin_i[0:1, 0:1], f2))
            f3 = c("f3")
            link(dve.tensor_scalar(c("g1"), ps[:, 5, NG:NG + 1], 1.0, None, ALU.is_lt))
            link(dve.tensor_scalar(c("g2"), ps[:, 5, NG + 1:NG + 2], 3.0, None, ALU.is_lt))
            link(dve.tensor_tensor(f3, c("g1"), c("g2"), ALU.mult))
            link(dve.tensor_scalar(basebc[:], basebc[:], f3, None, ALU.mult))
            dve.tensor_scalar(base_i[:], basebc[0:1, :], 0.5, None, ALU.mult).then_inc(table_ready, 1)

            def find_q(step):
                bb = basebc[0:TP].rearrange("p (a g) -> p a g", a=1).to_broadcast([TP, CK, NG])
                qv = q[0:TP]
                step(dve.tensor_tensor(qv, dv, bb, ALU.subtract))
                step(dve.tensor_scalar(tmp, qv, 0.0, None, ALU.is_ge))
                step(dve.scalar_tensor_tensor(tmp, qv, float(WIN), tmp, ALU.is_lt, ALU.mult))
                step(dve.tensor_tensor(qv, qv, hiv, ALU.add))
                step(dve.tensor_tensor(qv, qv, tmp, ALU.mult))
                step(dve.tensor_scalar(qv, qv, -1.0, None, ALU.add))

            tmp = inside[0:TP]
            find_q(link)
            nwin = dve.value_load(nwin_i[0:1, 0:1], min_val=1, max_val=NWIN)

            def onehots(s, r, g, first):
                if not first:
                    dve.wait_ge(counts_ready, s - 1)
                for k in range(CK):
                    dve.tensor_scalar(lohot[0:TP, r, k, 0:TP], iota_lo[0:TP, 0:TP], lo[0:TP, k, bass.ds(g, 1)],
                                      None, ALU.is_equal)
                    ins = dve.tensor_scalar(qhot[0:TP, r, k, :], iota_q[0:TP, :], q[0:TP, k, bass.ds(g, 1)],
                                            None, ALU.is_equal)
                ins.then_inc(onehots_made, 1)

            def pair(i):
                for r in range(2):
                    onehots(2 * i + r, r, 2 * i + r, isinstance(i, int) and i == 0)

            pair(0)
            with dve.Fori(1, EARLY) as i:
                pair(i)

            MC = {"x": 0} | {n: JT + m * (KT // 2) for m, n in enumerate(SPLIT)}

            def pow2(name, source):
                link(dve.tensor_scalar(c("t_" + name), source, 2.0 ** -40, None, ALU.max))
                link(dve.tensor_scalar(c("p_" + name).bitcast(I32), c("t_" + name).bitcast(I32), 0x7F800000, None,
                                       ALU.bitwise_and))
                link(dve.reciprocal(c("r_" + name), c("p_" + name)))

            def scale(name):
                n = ORDER.index(name)
                dve.wait_ge(max_spread, n + 1)
                pow2(name, c("all" + name))
                ins = dve.tensor_scalar(c("s_" + name), c("r_" + name), 8192.0, None, ALU.mult)
                own[0] += 1
                ins.then_inc(dve_step, 1)
                dve.wait_ge(dve_step, own[0])

            def signal(s):
                dve.sem_inc(s, 1)

            def tensor_max(name, n, cols):
                dve.tensor_reduce(c("max" + name), mx[:, cols:cols + n], AX.X, ALU.max).then_inc(maxes_ready, 1)

            def wmax(name, k):
                if name == "wn0":
                    dve.wait_ge(wn0_in[k // 2], 16)
                else:
                    dve.wait_ge(w_in[name], 16 * KT // 2)
                dve.tensor_reduce(mx[:, bass.ds(MC[name] + k // 2, 1)],
                                  WN[name][0][:, bass.ds(k + 1, 2)].rearrange("p k h d -> p (k h d)").bitcast(F32),
                                  AX.X, ALU.max, apply_absolute_value=True).then_inc(max_done, 1)

            def lsplit(name, k):
                n = SPLIT.index(name)
                dve.wait_ge(w_high, n * KT + k + 1)
                w = WN[name][0]
                dve.scalar_tensor_tensor(w[:, bass.ds(k, 1), 1, :].rearrange("p k d -> p (k d)"),
                                         w[:, bass.ds(k + 1, 1)].rearrange("p k h d -> p (k h d)").bitcast(F32),
                                         c("s_" + name),
                                         w[:, bass.ds(k, 1), 0, :].rearrange("p k d -> p (k d)"),
                                         ALU.mult, ALU.subtract).then_inc(w_low, 1)

            for j in range(JT):
                dve.wait_ge(x_in[j], 16)
                dve.tensor_reduce(mx[0:TP, j:j + 1], xraw[0:TP, j, :],
                                  AX.X, ALU.max, apply_absolute_value=True).then_inc(max_done, 1)
            dve.wait_ge(max_done, JT)
            tensor_max("x", JT, 0)
            for k in range(0, KT, 2):
                wmax("wn0", k)
            dve.wait_ge(max_done, JT + KT // 2)
            tensor_max("wn0", KT // 2, MC["wn0"])
            dve.wait_ge(b0_in, 16)
            dve.tensor_reduce(c("maxb0"), b0c[:], AX.X, ALU.max, apply_absolute_value=True).then_inc(maxes_ready, 1)
            scale("x")
            signal(scale_ready)
            scale("wn0")
            signal(scale_ready)
            for j in range(JT):
                dve.wait_ge(high_ready, j + 1)
                dve.scalar_tensor_tensor(xT[1][:, :, j * TP:(j + 1) * TP],
                                         bank(2 * (j % 2)).rearrange("p (k n) -> p k n", n=P)[:, :, 0:TP],
                                         c("s_x"), xT[0][:, :, j * TP:(j + 1) * TP],
                                         ALU.mult, ALU.subtract).then_inc(panel_out, 1)
            for k in range(KT):
                lsplit("wn0", k)

            def low(t, r, layer):
                dve.wait_ge(high_ready, (1 + layer) * JT + t + 1)
                p = bank(2 * r)[0:TP]
                if layer == 0:
                    dve.scalar_tensor_tensor(zh[0:TP, 1:KT + 1, 1, bass.ds(t * P, P)],
                                             p.rearrange("p (f c) -> p f c", f=KT), 2.0 ** -23,
                                             zh[0:TP, 1:KT + 1, 0, bass.ds(t * P, P)],
                                             ALU.mult, ALU.subtract).then_inc(panel_out, 1)
                else:
                    dve.scalar_tensor_tensor(z1[1][:, bass.ds(t, 1), :].rearrange("p j d -> p (j d)"), p,
                                             c("s_z1", TP), z1[0][:, bass.ds(t, 1), :].rearrange("p j d -> p (j d)"),
                                             ALU.mult, ALU.subtract).then_inc(panel_out, 1)

            def groups(i, extra, layer=0):
                for r in range(2):
                    t = 2 * i + r
                    for g in range(GT):
                        if layer == 0:
                            s = 2 * EARLY + t * GT + g
                            onehots(s, g % 2, s, False)
                        if g == 1 and not (isinstance(i, int) and t == 0):
                            low(t - 1, 1 - r, layer)
                        if g in (2, 4):
                            extra(i, 2 * r + g // 2 - 1)

            def nothing(i, m):
                pass

            groups(0, lambda i, m: wmax("ws0", 2 * m) if m < 2 else None)
            groups(1, lambda i, m: wmax("ws0", 4 + 2 * m) if m < 2 else None)
            dve.wait_ge(max_done, JT + 2 * (KT // 2))
            tensor_max("ws0", KT // 2, MC["ws0"])
            scale("ws0")
            signal(scale_ready)
            with dve.Fori(2, 4) as i:
                groups(i, lambda i, m: lsplit("ws0", 4 * i - 8 + m))
            groups(4, nothing)
            low(JT - 1, 1, 0)

            with dve.If(nwin > 1):
                with dve.Fori(1, nwin) as w:
                    dve.wait_ge(onehots_made, w * NG)
                    n_step = [0]

                    def step(ins):
                        n_step[0] += 1
                        ins.then_inc(win_step, 1)
                        dve.wait_ge(win_step, (w - 1) * 7 + n_step[0])

                    step(dve.tensor_scalar(basebc[:], basebc[:], float(WIN), None, ALU.add))
                    find_q(step)
                    apart(dve)
                    with dve.Fori(0, PAIRS) as i:
                        for r in range(2):
                            onehots(w * NG + 2 * i + r, r, 2 * i + r, False)

            dve.wait_ge(counts_added, nwin * NG)
            dve.tensor_copy(AF[0:TP], A[0:TP]).then_inc(A_ready, 1)

            def mul(o, a, b, f=1.0):
                link(dve.scalar_tensor_tensor(c(o), c(a), f, c(b), ALU.mult, ALU.mult))

            link(dve.tensor_tensor(c("pw"), c("p_wn0"), c("p_ws0"), ALU.add))
            mul("bound", "p_x", "pw", 4096.0)
            dve.wait_ge(max_spread, ORDER.index("b0") + 1)
            link(dve.tensor_tensor(c("bound"), c("bound"), c("allb0"), ALU.add))
            pow2("h", c("bound"))
            link(dve.tensor_scalar(c("s_h"), c("r_h"), 2.0 ** 14, None, ALU.mult))
            mul("cs", "p_x", "p_ws0", 2.0 ** -26)
            mul("cs", "cs", "s_h")
            mul("ca", "p_x", "p_wn0", 2.0 ** -3)
            mul("ca", "ca", "s_h")
            link(dve.tensor_scalar(b0h[:], b0c[:], c("s_h"), None, ALU.mult))
            for n in range(3):
                dve.wait_ge(deg_ready, n + 1)
                link(dve.tensor_scalar(dinvbc[:, CO[n]:CO[n] + CH[n]], ps[:, (6, 7, 5)[n], 0:CH[n]], 1.0, None,
                                       ALU.max))
            link(dve.reciprocal(dinvbc[:], dinvbc[:]))
            dp = dprod[0:TP].rearrange("p (j n) -> p j n", j=JT)
            link(dve.tensor_tensor(dp, dinvbc[0:TP].rearrange("p (j n) -> p j n", j=JT),
                                   ident[0:TP, 0:TP].rearrange("p (a n) -> p a n", a=1).to_broadcast([TP, JT, TP]),
                                   ALU.mult))
            link(dve.tensor_reduce(dinvT[0:TP], dp, AX.X, ALU.add))
            link(dve.tensor_scalar(dinvbc[:], dinvbc[:], c("ca"), None, ALU.mult))
            signal(dinv_ready)

            def hlow(f, n):
                dve.wait_ge(h_high, 3 * f + n + 1)
                dve.tensor_reduce(hmx[:, bass.ds(3 * f + n, 1)], h32[:, n, 0:CH[n]], AX.X, ALU.max)
                dve.tensor_tensor(zflat[:, bass.ds((2 * f + 1) * BLK + CO[n], CH[n])], h32[:, n, 0:CH[n]],
                                  zflat[:, bass.ds(2 * f * BLK + CO[n], CH[n])], ALU.subtract).then_inc(h_low, 1)

            def unit(f, n):
                v = 3 * f + n
                dve.wait_ge(unit_ready, v + 1)
                dve.tensor_tensor(pre[:, n, 0:CH[n]], ps[:, n, 0:CH[n]], dinvbc[:, CO[n]:CO[n] + CH[n]],
                                  ALU.mult).then_inc(dsum, 1)
                dve.wait_ge(dsum, v + 1)
                dve.scalar_tensor_tensor(pre[:, n, 0:CH[n]], ps[:, 3 + n, 0:CH[n]], c("cs"), pre[:, n, 0:CH[n]],
                                         ALU.mult, ALU.add).then_inc(pre_ready, 1)

            def units(f):
                for n in range(3):
                    unit(f, n)
                    if n:
                        hlow(f, n - 1)
                    elif not (isinstance(f, int) and f == 0):
                        hlow(f - 1, 2)

            units(0)
            wmax("wn1", 0)
            with dve.Fori(1, KT // 2) as f:
                units(f)
                wmax("wn1", 2 * f)
            dve.wait_ge(max_done, JT + 3 * (KT // 2))
            tensor_max("wn1", KT // 2, MC["wn1"])
            scale("wn1")
            signal(scale_ready)
            with dve.Fori(KT // 2, KT) as f:
                units(f)
                for k in range(2):
                    lsplit("wn1", 2 * f - KT + k)
            hlow(KT - 1, 2)
            dve.wait_ge(h_low, 3 * KT)

            dve.tensor_reduce(c("maxh"), hmx[:], AX.X, ALU.max).then_inc(maxes_ready, 1)
            dve.wait_ge(max_spread, ORDER.index("h") + 1)
            pow2("hs", c("allh"))
            link(dve.tensor_scalar(c("s_z1"), c("r_hs"), 2.0 ** -10, None, ALU.mult))
            signal(scale_ready)
            mul("ca1", "p_h", "p_wn1", 2.0 ** -17)
            mul("ca1", "ca1", "p_hs")
            link(dve.tensor_scalar(dinvT[0:TP], dinvT[0:TP], c("ca1", TP), None, ALU.mult))

            groups(0, lambda i, m: wmax("ws1", 2 * m) if m < 2 else None, 1)
            groups(1, lambda i, m: wmax("ws1", 4 + 2 * m) if m < 2 else None, 1)
            dve.wait_ge(max_done, JT + 4 * (KT // 2))
            tensor_max("ws1", KT // 2, MC["ws1"])
            scale("ws1")
            signal(scale_ready)
            mul("cs1", "p_h", "p_ws1", 2.0 ** -27)
            with dve.Fori(2, 4) as i:
                groups(i, lambda i, m: lsplit("ws1", 4 * i - 8 + m), 1)
            groups(4, nothing, 1)
            low(JT - 1, 1, 1)

            def finish(i, r, first):
                t = 2 * i + r
                g = 4 * (1 - r)
                y = ybuf[r]
                dve.wait_ge(xb_ready, t + 1)
                dve.wait_ge(out_ready, t + 1)
                if not first:
                    dve.wait_ge(o_ready, t - 1)
                dve.scalar_tensor_tensor(y, bank(g + 2)[0:TP], dinvT[0:TP, bass.ds(t, 1)], xres[r],
                                         ALU.mult, ALU.add).then_inc(y_part, 1)
                dve.wait_ge(y_part, t + 1)
                dve.scalar_tensor_tensor(y, bank(g)[0:TP], c("cs1", TP), y, ALU.mult, ALU.add).then_inc(y_ready, 1)
                dve.wait_ge(y_ready, t + 1)
                for h in range(2):
                    ins = dve.bn_stats(st[0:TP, r, 6 * h:6 * h + 6], y[:, h * HD:(h + 1) * HD])
                ins.then_inc(stat_ready, 1)
                dve.wait_ge(stat_ready, t + 1)
                apart(dve)
                dve.bn_aggr(mv[0:TP, r, :], st[0:TP, r, :]).then_inc(aggr_ready, 1)
                dve.wait_ge(aggr_ready, t + 1)
                dve.tensor_scalar(ln[0:TP, r, 0:1], mv[0:TP, r, 1:2], 1e-5, None, ALU.add).then_inc(var_ready, 1)
                dve.wait_ge(std_ready, t + 1)
                dve.reciprocal(ln[0:TP, r, 2:3], ln[0:TP, r, 1:2]).then_inc(rstd_ready, 1)
                dve.wait_ge(rstd_ready, t + 1)
                dve.scalar_tensor_tensor(ln[0:TP, r, 3:4], mv[0:TP, r, 0:1], -1.0, ln[0:TP, r, 2:3],
                                         ALU.mult, ALU.mult).then_inc(shift_ready, 1)

            finish(0, 0, True)
            finish(0, 1, True)
            with dve.Fori(1, IT) as i:
                for r in range(2):
                    finish(i, r, False)


_INS = ["x", "src", "dst", "L0_gnn_W_neigh0", "L0_gnn_W_self0", "L0_gnn_b0", "L0_gnn_W_neigh1", "L0_gnn_W_self1",
        "L0_gnn_b1"]


def kernel(**inputs):
    import numpy as _np
    import concourse.bacc as _bacc
    from concourse import mybir as _mybir
    from concourse.bass_utils import run_bass_kernel_spmd as _run

    nc = _bacc.Bacc("TRN2", target_bir_lowering=False, num_devices=1)
    arrays, args = {}, []
    for name in _INS:
        a = _np.ascontiguousarray(inputs[name])
        arrays[f"in_{name}"] = a
        args.append(nc.dram_tensor(f"in_{name}", a.shape, _mybir.dt.from_np(a.dtype), kind="ExternalInput").ap())
    args.append(nc.dram_tensor("out_0", inputs["x"].shape, _mybir.dt.float32, kind="ExternalOutput").ap())
    gnn_kernel(nc, *args)
    r = _run(nc, [arrays], core_ids=[0])
    return r.results[0]["out_0"]
```

```python
from contextlib import ExitStack

import concourse.bass as bass
from concourse import mybir

ALU = mybir.AluOpType
ACT = mybir.ActivationFunctionType
AX = mybir.AxisListType
F32 = mybir.dt.float32
F16 = mybir.dt.float16
I32 = mybir.dt.int32
U16 = mybir.dt.uint16
RMAX = bass.bass_isa.ReduceOp.max

P = 128
WIN = 24
CK = 2
GR = 2
RING = 4
ZK = 2 * P


def gnn_kernel(nc, x, src, dst, Wn0, Ws0, b0, Wn1, Ws1, b1, out):
    N, D = x.shape
    E = src.shape[0]
    TP = 125
    JT = N // TP
    KT = D // P
    HD = D // 2
    GE = CK * TP
    NG = E // GE
    NWIN = -(-N // WIN)
    NPAD = NWIN * WIN
    HN = JT * WIN
    assert N == TP * JT and D == P * KT and E == GE * NG and HD <= 512 and HN <= 512
    CH = [420, 420, N - 840]
    CO = [0, 420, 840]
    DEG = (6, 7, 2)
    SELF = (4, 5, 3)
    BLK = JT * P
    RE = GR * GE
    NR = NG // GR
    GT = NG // JT
    EARLY = GT
    GK = GT // KT
    IT = JT // 2
    SAME = 7
    assert GT == GK * KT and GT % RING == 0 and NR * RE == E and SAME * GE <= 2048 - 2 * (GE - 1) + GE

    with ExitStack() as ctx:
        def sb(name, shape, dt):
            return ctx.enter_context(nc.sbuf_tensor(name, shape, dt))

        def sem(name):
            return ctx.enter_context(nc.semaphore(name))

        xz = sb("xz", [P, 2 * JT * D], F16)
        zh = sb("zh", [P, KT + 1, 2, BLK], F16)
        wn = sb("wn", [P, KT + 1, 2, D], F16)
        ws = sb("ws", [P, KT + 1, 2, D], F16)
        A = sb("A", [P, JT, NPAD], U16)
        scratch = sb("scratch", [P, 5120], F16)
        lohot = sb("lohot", [P, RING, CK, P], F16)
        table = sb("table", [P, 5, GR * CK, NR], F32)
        basebc = sb("basebc", [P, GR, NR], F32)
        base_i = sb("base_i", [1, GR * NR], I32)
        iota_lo = sb("iota_lo", [P, P], F16)
        iota_q = sb("iota_q", [P, HN], F16)
        ident = sb("ident", [P, P], F32)
        ones = sb("ones", [P, P], F32)
        ones16 = sb("ones16", [P, P], F16)
        dinvT = sb("dinvT", [P, JT], F32)
        b0c = sb("b0c", [P, KT], F32)
        b0h = sb("b0h", [P, KT], F32)
        mx = sb("mx", [P, 5 * KT + 16], F32)
        hmx = sb("hmx", [P, 3 * KT], F32)
        S = sb("S", [P, 64], F32)
        nwin_i = sb("nwin_i", [1, 2], I32)
        SG = sb("SG", [P, 4, GR], F32)
        fl = sb("fl", [P, 6], F32)
        st = sb("st", [P, 2, 12], F32)
        mv = sb("mv", [P, 2, 2], F32)
        ln = sb("ln", [P, 2, 4], F32)
        ps = ctx.enter_context(nc.psum_tensor("ps", [P, 8, 512], F32))

        xT = [xz[:, i * KT * N:(i + 1) * KT * N].rearrange("p (k n) -> p k n", k=KT) for i in range(2)]
        z1 = [xz[0:TP, i * JT * D:(i + 1) * JT * D].rearrange("p (j d) -> p j d", j=JT) for i in range(2)]
        zflat = zh[:].rearrange("p k h n -> p (k h n)")
        xraw = zflat[:, 0:2 * JT * D].bitcast(F32).rearrange("p (j d) -> p j d", j=JT)
        lo, q, hi, dcol, inside = (table[:, i] for i in range(5))
        dinvbc = table[:].rearrange("p a k g -> p (a k g)")[:, 0:N]
        AF = A[:].bitcast(F16)
        A32 = A[:].bitcast(I32)
        QH = RING * CK * HN
        qhot = scratch[:, 0:QH].rearrange("p (s c n) -> p s c n", s=RING, c=CK)
        stage = scratch[:, QH:QH + RING * HN].bitcast(U16).rearrange("p (s j w) -> p s j w", s=RING, j=JT)
        stage32 = scratch[:, QH:QH + RING * HN].bitcast(I32).rearrange("p (s j w) -> p s j w", s=RING, j=JT)
        pre = scratch[:, 0:2 * 3 * 420].bitcast(F32).rearrange("p (n c) -> p n c", n=3)
        h32 = scratch[:, 2 * 3 * 420:4 * 3 * 420].bitcast(F32).rearrange("p (n c) -> p n c", n=3)
        dp = scratch[0:TP, 0:2 * N].bitcast(F32).rearrange("p (j n) -> p j n", j=JT)
        eraw = xz[0:NR, 0:4 * RE].bitcast(I32).rearrange("p (t e) -> p t e", t=2)
        ef = xz[0:NR, 4 * RE:8 * RE].bitcast(F32).rearrange("p (t e) -> p t e", t=2)
        NF = GR * NR + 2 * GR
        eb = xz[0:NR, 8 * RE:8 * RE + 2 * NF].bitcast(F32)
        unread = xz[:, 16 * D:17 * D]
        wnf = wn[:].rearrange("p k h d -> p k (h d)").bitcast(F32)
        b1bc = wnf[0:TP, 0, :]
        xres = [wnf[0:TP, 1 + i, :] for i in range(2)]
        ybuf = [wnf[0:TP, 3 + i, :] for i in range(2)]
        obuf = [wnf[0:TP, 5 + i, :] for i in range(2)]

        def raw(w, k, n=1):
            return w[:, k + 1:k + 1 + n].rearrange("p k h d -> p k (h d)").bitcast(F32)

        def bank(b, n=2):
            return ps[:, b:b + n, :].rearrange("p b c -> p (b c)")

        col = {}

        def c(name, rows=P):
            i = col.setdefault(name, len(col))
            assert i < 64, name
            return S[0:rows, i:i + 1]

        edges_in = sem("edges_in")
        x_in = [sem(f"x_in{j}") for j in range(JT)]
        wn0_in = [sem(f"wn0_in{k}") for k in range(KT // 2)]
        w_in = {n: sem(f"{n}_in") for n in ("ws0", "wn1", "ws1")}
        b0_in = sem("b0_in")
        b1_in = sem("b1_in")
        consts_ready = sem("consts_ready")
        dve_step = sem("dve_step")
        pool_step = sem("pool_step")
        edges_float = sem("edges_float")
        edges_turned = sem("edges_turned")
        edges_diag = sem("edges_diag")
        edges_spread = sem("edges_spread")
        table_ready = sem("table_ready")
        onehots_made = sem("onehots_made")
        counts_ready = sem("counts_ready")
        counts_copied = sem("counts_copied")
        counts_added = sem("counts_added")
        passed = sem("passed")
        sums_done = sem("sums_done")
        win_step = sem("win_step")
        max_done = sem("max_done")
        maxes_ready = sem("maxes_ready")
        max_spread = sem("max_spread")
        scale_ready = sem("scale_ready")
        panel_ready = sem("panel_ready")
        high_ready = sem("high_ready")
        panel_out = sem("panel_out")
        w_high = sem("w_high")
        w_low = sem("w_low")
        A_ready = sem("A_ready")
        deg_ready = sem("deg_ready")
        dinv_diag = sem("dinv_diag")
        dinv_spread = sem("dinv_spread")
        dinv_ready = sem("dinv_ready")
        unit_ready = sem("unit_ready")
        pre_ready = sem("pre_ready")
        dsum = sem("dsum")
        h32_ready = sem("h32_ready")
        h_high = sem("h_high")
        h_low = sem("h_low")
        hmax_done = sem("hmax_done")
        out_ready = sem("out_ready")
        x_again = [sem(f"x_again{i}") for i in range(2)]
        xb_ready = sem("xb_ready")
        y_part = sem("y_part")
        y_ready = sem("y_ready")
        stat_ready = sem("stat_ready")
        aggr_ready = sem("aggr_ready")
        var_ready = sem("var_ready")
        std_ready = sem("std_ready")
        rstd_ready = sem("rstd_ready")
        shift_ready = sem("shift_ready")
        o_ready = sem("o_ready")
        o_stored = [sem(f"o_stored{i}") for i in range(2)]

        block = ctx.enter_context(nc.Block())

        WN = {"wn0": (wn, ws, Wn0), "ws0": (ws, ws, Ws0), "wn1": (wn, wn, Wn1), "ws1": (ws, ws, Ws1)}
        ORDER = ["x", "wn0", "b0", "ws0", "wn1", "h", "ws1"]
        SPLIT = ["wn0", "ws0", "wn1", "ws1"]

        MC = {"x": 0} | {n: JT + KT * m for m, n in enumerate(SPLIT)}

        def load_weights(eng, name):
            _, buf, dram = WN[name]
            d = dram.rearrange("(k p) d -> p k d", p=P)
            for k in range(0, KT, 2):
                landed = wn0_in[k // 2] if name == "wn0" else w_in[name]
                eng.dma_start(raw(buf, k, 2), d[:, k:k + 2, :]).then_inc(landed, 16)

        def apart(eng):
            eng.sem_inc(passed, 1)

        @block.sync
        def _(sp):
            sp.dma_start(eraw[:, 0, :], dst.rearrange("(g e) -> g e", e=RE)).then_inc(edges_in, 16)
            sp.dma_start(eraw[:, 1, :], src.rearrange("(g e) -> g e", e=RE)).then_inc(edges_in, 16)
            for j in range(JT):
                sp.dma_start(xraw[0:TP, j, :], x[j * TP:(j + 1) * TP, :]).then_inc(x_in[j], 16)
            load_weights(sp, "wn0")
            sp.dma_start(b0c[:], b0.rearrange("(f p) -> p f", p=P), allow_slow_non_contiguous=True).then_inc(b0_in, 16)
            sp.wait_ge(w_low, KT)
            load_weights(sp, "ws0")
            sp.wait_ge(panel_ready, 2 * JT)
            load_weights(sp, "wn1")
            sp.wait_ge(unit_ready, 3 * KT)
            load_weights(sp, "ws1")
            sp.wait_ge(panel_ready, 3 * JT)
            sp.dma_start(b1bc, b1.rearrange("(a d) -> a d", a=1).to_broadcast([TP, D])).then_inc(b1_in, 16)

            def rows(i):
                for r in range(2):
                    t = 2 * i + r
                    if not isinstance(i, int) or i >= 1:
                        sp.wait_ge(y_part, t - 1)
                    sp.dma_start(xres[r], x[bass.ds(t * TP, TP), :]).then_inc(x_again[r], 16)

            rows(0)
            with sp.Fori(1, IT) as i:
                rows(i)

        @block.gpsimd
        def _(pool):
            own = [0]

            def link(ins):
                own[0] += 1
                ins.then_inc(pool_step, 1)
                pool.wait_ge(pool_step, own[0])

            link(pool.memset(ones[:], 1.0))
            link(pool.memset(ones16[:], 1.0))
            link(pool.affine_select(out=ident[:], in_=ones[:], compare_op=ALU.is_equal, fill=0.0, base=0,
                                    pattern=[[-1, P]], channel_multiplier=1))
            link(pool.memset(mx[:], 0.0))
            pool.iota(iota_lo[:], [[1, P]], base=0, channel_multiplier=0,
                      allow_small_or_imprecise_dtypes=True).then_inc(consts_ready, 1)
            pool.iota(iota_q[:], [[1, HN]], base=0, channel_multiplier=0,
                      allow_small_or_imprecise_dtypes=True).then_inc(consts_ready, 1)
            pool.wait_ge(table_ready, 1)
            nwin = pool.value_load(nwin_i[0:1, 0:1], min_val=1, max_val=NWIN)

            def add(s, r, first, base):
                if not first:
                    pool.wait_ge(counts_added, s)
                pool.wait_ge(counts_copied, s + 1)
                apart(pool)
                a = A32[0:TP, :, bass.ds(base, WIN // 2)]
                pool.tensor_tensor(a, a, stage32[0:TP, r], ALU.add).then_inc(counts_added, 1)

            def ring(i):
                _, bases = nc.values_load_multi_w_load_instructions(
                    base_i[0:1, bass.ds(RING * i, RING)], engines=[pool.engine], min_val=0,
                    max_val=(NPAD - WIN) // 2, skip_runtime_bounds_check_because="clamped where it is computed")
                for r in range(RING):
                    add(RING * i + r, r, isinstance(i, int) and i == 0 and r == 0, bases[r])

            def spread(n):
                pool.wait_ge(maxes_ready, n + 1)
                pool.partition_all_reduce(c("all" + ORDER[n]), c("max" + ORDER[n]), P, RMAX).then_inc(max_spread, 1)

            ring(0)
            ring(1)
            spread(0)
            with pool.Fori(2, EARLY // RING) as i:
                ring(i)
            spread(1)
            spread(2)
            with pool.Fori(EARLY // RING, (EARLY + 4 * GT) // RING) as i:
                ring(i)
            spread(3)
            with pool.Fori((EARLY + 4 * GT) // RING, NG // RING) as i:
                ring(i)
            with pool.If(nwin > 1):
                with pool.Fori(1, nwin) as w:
                    with pool.Fori(0, NG // RING) as i:
                        for r in range(RING):
                            add(w * NG + RING * i + r, r, False, w * (WIN // 2))
            for n in range(4, 7):
                spread(n)
            pool.wait_ge(b1_in, 16)

            def residual(i):
                for r in range(2):
                    pool.wait_ge(x_again[r], 16 * (i + 1))
                    pool.tensor_tensor(xres[r], xres[r], b1bc, ALU.add).then_inc(xb_ready, 1)

            with pool.Fori(0, IT) as i:
                residual(i)

        @block.tensor
        def _(pe):
            pe.wait_ge(consts_ready, 2)
            for t in range(2):
                pe.wait_ge(edges_float, t + 1)
                for b in range(GR * CK):
                    ins = pe.transpose(ps[0:TP, 6 + t, b * NR:(b + 1) * NR], ef[:, t, b * TP:(b + 1) * TP],
                                       ident[0:NR, 0:NR])
                ins.then_inc(edges_turned, 1)
            pe.wait_ge(edges_diag, 1)
            pe.matmul(ps[:, 5, 0:NF], ones[0:NR, :], eb[:, 0:NF], start=True, stop=True).then_inc(
                edges_spread, 1)

            def count(s, r, banks):
                pe.wait_ge(onehots_made, s + 1)
                if not (isinstance(s, int) and s < banks):
                    pe.wait_ge(counts_copied, s - banks + 1)
                for k in range(CK):
                    ins = pe.matmul(ps[0:TP, 8 - banks + r % banks, 0:HN], lohot[0:TP, r, k, 0:TP], qhot[0:TP, r, k, :],
                                    start=(k == 0), stop=(k == CK - 1))
                ins.then_inc(counts_ready, 1)

            for s in range(EARLY):
                count(s, s % RING, 2)
            for j in range(JT):
                pe.wait_ge(x_in[j], 16)
                if j == 2:
                    pe.wait_ge(table_ready, 1)
                if j >= 3:
                    pe.wait_ge(panel_out, j - 2)
                for k in range(KT):
                    b, o = divmod(k * P, 512)
                    ins = pe.transpose(ps[:, 2 * (j % 3) + b, o:o + TP], xraw[0:TP, j, k * P:(k + 1) * P],
                                       ident[0:TP, 0:TP])
                ins.then_inc(panel_ready, 1)

            def panel(i, r, lhs, w, layer):
                t = 2 * i + r
                pe.wait_ge(panel_out, (1 + layer) * JT + t - 1)
                if layer == 1 and isinstance(t, int) and t == 1:
                    pe.wait_ge(pre_ready, 3 * KT)
                for k in range(KT):
                    if layer == 0:
                        if isinstance(i, int) and t == 0:
                            pe.wait_ge(w_low, k + 1)
                        for g in range(GK):
                            if not (isinstance(t, int) and t == JT - 1):
                                count(EARLY + t * GT + k * GK + g, (k * GK + g) % RING, RING)
                    elif isinstance(i, int) and t == 0:
                        pe.wait_ge(h_low, 3 * (k + 1))
                    for a, bs in ((0, (0, 1)), (1, (0,))):
                        for b in bs:
                            for half in range(2):
                                ins = pe.matmul(ps[0:TP, 2 * r + half, :], lhs(a, k, t),
                                                w[:, k, b, half * HD:(half + 1) * HD],
                                                start=(k == 0 and a == 0 and b == 0),
                                                stop=(k == KT - 1 and a == 1))
                ins.then_inc(panel_ready, 1)

            def node_tiles(lhs, w, layer):
                for r in range(2):
                    panel(0, r, lhs, w, layer)
                with pe.Fori(1, IT - 1 + layer) as i:
                    for r in range(2):
                        panel(i, r, lhs, w, layer)
                if layer == 0:
                    for r in range(2):
                        panel(IT - 1, r, lhs, w, layer)

            pe.wait_ge(table_ready, 1)
            nwin = pe.value_load(nwin_i[0:1, 0:1], min_val=1, max_val=NWIN)
            pe.wait_ge(panel_out, JT)
            node_tiles(lambda a, k, t: xT[a][:, k, bass.ds(t * TP, TP)], wn, 0)
            with pe.If(nwin > 1):
                with pe.Fori(1, nwin) as w:
                    with pe.Fori(0, NG // RING) as i:
                        for r in range(RING):
                            count(w * NG + RING * i + r, r, RING)

            def self_part(f, n):
                if not isinstance(f, int):
                    pe.wait_ge(pre_ready, 3 * f + n - 2)
                for k in range(KT):
                    for a, b in ((0, 0), (0, 1), (1, 0)):
                        pe.matmul(ps[:, SELF[n], 0:CH[n]], ws[:, k, a, bass.ds(f * P, P)],
                                  xT[b][:, k, CO[n]:CO[n] + CH[n]],
                                  start=(k == 0 and a == 0 and b == 0), stop=(k == KT - 1 and a == 1))

            def neighbour_part(f, n):
                for j in range(JT):
                    for a in range(2):
                        ins = pe.matmul(ps[:, n, 0:CH[n]], zflat[0:TP, bass.ds((2 * f + 2 + a) * BLK + j * P, P)],
                                        AF[0:TP, j, CO[n]:CO[n] + CH[n]],
                                        start=(j == 0 and a == 0), stop=(j == JT - 1 and a == 1))
                ins.then_inc(unit_ready, 1)

            pe.wait_ge(w_low, 2 * KT)
            pe.wait_ge(counts_copied, nwin * NG)
            for n in range(3):
                if n == 2:
                    pe.wait_ge(panel_out, 2 * JT)
                self_part(0, n)
            pe.wait_ge(A_ready, 1)
            for t in range(JT):
                for j in range(JT):
                    ins = pe.matmul(ps[0:TP, 6, t:t + 1], AF[0:TP, j, t * TP:(t + 1) * TP], ones16[0:TP, 0:1],
                                    start=(j == 0), stop=(j == JT - 1))
            ins.then_inc(deg_ready, 1)
            neighbour_part(0, 0)
            pe.wait_ge(dinv_diag, 1)
            for n in range(3):
                for t in range(4 * n, min(4 * n + 4, JT)):
                    ins = pe.matmul(ps[:, DEG[n], (t % 4) * TP:(t % 4 + 1) * TP], ones[0:TP, :], dp[:, t, :],
                                    start=True, stop=True)
                ins.then_inc(dinv_spread, 1)
            neighbour_part(0, 1)
            pe.wait_ge(dinv_ready, 1)
            neighbour_part(0, 2)
            with pe.Fori(1, KT) as f:
                for n in range(3):
                    self_part(f, n)
                    neighbour_part(f, n)

            pe.wait_ge(w_low, 3 * KT)
            pe.wait_ge(pre_ready, 3 * KT - 1)
            node_tiles(lambda a, k, t: zh[:, k, a, bass.ds(t * TP, TP)], wn, 1)

            pe.wait_ge(w_low, 4 * KT)

            def tile(i, r, first):
                t = 2 * i + r
                g = 4 * (1 - r)
                if not first:
                    pe.wait_ge(y_ready, t - 1)
                elif r == 1:
                    pe.wait_ge(panel_out, 3 * JT)
                for k in range(KT):
                    for a, bs in ((0, (0, 1)), (1, (0,))):
                        for b in bs:
                            for half in range(2):
                                pe.matmul(ps[0:TP, g + half, :], zh[:, k, a, bass.ds(t * TP, TP)],
                                          ws[:, k, b, half * HD:(half + 1) * HD],
                                          start=(k == 0 and a == 0 and b == 0), stop=(k == KT - 1 and a == 1))
                if first and r == 0:
                    pe.wait_ge(panel_out, 3 * JT)
                for j in range(JT):
                    for b in range(2):
                        for half in range(2):
                            ins = pe.matmul(ps[0:TP, g + 2 + half, :], AF[0:TP, j, bass.ds(t * TP, TP)],
                                            z1[b][:, j, half * HD:(half + 1) * HD],
                                            start=(j == 0 and b == 0), stop=(j == JT - 1 and b == 1))
                ins.then_inc(out_ready, 1)

            tile(0, 0, True)
            tile(0, 1, True)
            with pe.Fori(1, IT) as i:
                for r in range(2):
                    tile(i, r, False)

        @block.scalar
        def _(act):
            def take(s, r, banks):
                act.wait_ge(counts_ready, s + 1)
                if not (isinstance(s, int) and s < RING):
                    act.wait_ge(counts_added, s - RING + 1)
                act.activation(stage[0:TP, r], ps[0:TP, 8 - banks + r % banks, 0:HN].rearrange("p (j w) -> p j w", j=JT),
                               ACT.Copy).then_inc(counts_copied, 1)

            act.wait_ge(consts_ready, 2)
            for j in range(JT):
                act.wait_ge(x_in[j], 16)
                act.activation(unread[0:TP], xraw[0:TP, j, :], ACT.Abs,
                               accum_out=mx[0:TP, j:j + 1]).then_inc(sums_done, 1)
                act.wait_ge(sums_done, j + 1)
                if j in (5, 6, 7):
                    for s in range(4 * (j - 5), 4 * (j - 4)):
                        take(s, s % RING, 2)
            for s in range(12, EARLY):
                take(s, s % RING, 2)

            act.wait_ge(scale_ready, 1)
            for j in range(JT):
                act.wait_ge(panel_ready, j + 1)
                act.activation(xT[0][:, :, j * TP:(j + 1) * TP],
                               bank(2 * (j % 3)).rearrange("p (k n) -> p k n", n=P)[:, :, 0:TP],
                               ACT.Copy, scale=c("s_x")).then_inc(high_ready, 1)
                if j in (2, 4, 6, 9):
                    n = (2, 4, 6, 9).index(j)
                    act.wait_ge(wn0_in[n], 16)
                    act.activation(wn[:, KT, 0, :], raw(ws, 2 * n + 1).rearrange("p k d -> p (k d)"), ACT.Abs,
                                   accum_out=mx[:, MC["wn0"] + 2 * n + 1:MC["wn0"] + 2 * n + 2]).then_inc(sums_done, 1)
                    act.wait_ge(sums_done, JT + n + 1)

            def split(name, k):
                n = SPLIT.index(name)
                if name != "wn0":
                    act.wait_ge(w_low, n * KT + k)
                w, wr, _ = WN[name]
                act.activation(w[:, bass.ds(k, 1), 0, :].rearrange("p k d -> p (k d)"),
                               wr[:, bass.ds(k + 1, 1)].rearrange("p k h d -> p (k h d)").bitcast(F32),
                               ACT.Copy, scale=c("s_" + name)).then_inc(w_high, 1)

            act.wait_ge(scale_ready, 2)
            for k in range(KT):
                split("wn0", k)

            def z0out(a, t):
                return zh[0:TP, 1:KT + 1, a, bass.ds(t * P, P)]

            def row_sums(k):
                act.wait_ge(w_in["ws0"], 16 * KT // 2)
                act.activation(wn[:, KT, 0, :], raw(ws, k).rearrange("p k d -> p (k d)"), ACT.Abs,
                               accum_out=mx[:, MC["ws0"] + k:MC["ws0"] + k + 1]).then_inc(sums_done, 1)
                act.wait_ge(sums_done, JT + KT // 2 + k + 1)

            def panels(i, layer, splits=None, sums=False):
                for r in range(2):
                    t = 2 * i + r
                    for g in range(GT):
                        if layer == 0 and not (isinstance(t, int) and t == JT - 1):
                            take(EARLY + t * GT + g, g % RING, RING)
                        if splits and g in (3, 9):
                            split(splits, 4 * i - 8 + 2 * r + g // 6)
                        if sums and g % 4 == 3:
                            row_sums(4 * r + g // 4)
                    act.wait_ge(panel_ready, (1 + layer) * JT + t + 1)
                    p = bank(2 * r)[0:TP]
                    if layer == 0:
                        act.activation(z0out(0, t), p.rearrange("p (f c) -> p f c", f=KT), ACT.Copy,
                                       scale=2.0 ** -13).then_inc(high_ready, 1)
                    else:
                        act.activation(z1[0][:, bass.ds(t, 1), :].rearrange("p j d -> p (j d)"), p, ACT.Copy,
                                       scale=c("s_z1", TP)).then_inc(high_ready, 1)

            panels(0, 0)
            panels(1, 0, sums=True)
            act.wait_ge(scale_ready, 3)
            with act.Fori(2, 4) as i:
                panels(i, 0, "ws0")
            panels(4, 0)
            act.wait_ge(table_ready, 1)
            nwin = act.value_load(nwin_i[0:1, 0:1], min_val=1, max_val=NWIN)
            with act.If(nwin > 1):
                with act.Fori(1, nwin) as w:
                    with act.Fori(0, NG // RING) as i:
                        for r in range(RING):
                            take(w * NG + RING * i + r, r, RING)

            act.wait_ge(dinv_ready, 1)

            def unit(f, n):
                v = 3 * f + n
                act.wait_ge(pre_ready, v + 1)
                apart(act)
                act.activation(h32[:, n, 0:CH[n]], pre[:, n, 0:CH[n]], ACT.Relu,
                               bias=b0h[:, bass.ds(f, 1)]).then_inc(h32_ready, 1)
                act.wait_ge(h32_ready, v + 1)
                act.activation(zflat[:, bass.ds(2 * f * BLK + CO[n], CH[n])], h32[:, n, 0:CH[n]],
                               ACT.Copy).then_inc(h_high, 1)

            with act.Fori(0, 3) as f:
                for n in range(3):
                    unit(f, n)
            act.wait_ge(scale_ready, 4)
            with act.Fori(3, KT - 1) as f:
                for n in range(3):
                    unit(f, n)
                for k in range(2):
                    split("wn1", 2 * f - 6 + k)
            for n in range(3):
                unit(KT - 1, n)

            act.wait_ge(scale_ready, 5)
            with act.Fori(0, 2) as i:
                panels(i, 1)
            act.wait_ge(scale_ready, 6)
            with act.Fori(2, 4) as i:
                panels(i, 1, "ws1")
            panels(4, 1)

            def finish(i, r, first):
                t = 2 * i + r
                act.wait_ge(var_ready, t + 1)
                act.activation(ln[0:TP, r, 1:2], ln[0:TP, r, 0:1], ACT.Sqrt).then_inc(std_ready, 1)
                act.wait_ge(shift_ready, t + 1)
                if not first:
                    act.wait_ge(o_stored[r], 16 * i)
                act.activation(obuf[r], ybuf[r], ACT.Identity, bias=ln[0:TP, r, 3:4],
                               scale=ln[0:TP, r, 2:3]).then_inc(o_ready, 1)
                act.wait_ge(o_ready, t + 1)
                act.dma_start(out[bass.ds(t * TP, TP), :], obuf[r]).then_inc(o_stored[r], 16)

            finish(0, 0, True)
            finish(0, 1, True)
            with act.Fori(1, IT) as i:
                for r in range(2):
                    finish(i, r, False)
            for r in range(2):
                act.wait_ge(o_stored[r], 16 * IT)

        @block.vector
        def _(dve):
            own = [0]

            def link(ins):
                own[0] += 1
                ins.then_inc(dve_step, 1)
                dve.wait_ge(dve_step, own[0])

            link(dve.memset(A[:].bitcast(I32), 0))
            dve.wait_ge(edges_in, 32)
            for t in range(2):
                dve.tensor_copy(ef[:, t, :], eraw[:, t, :]).then_inc(edges_float, 1)
            dve.wait_ge(edges_float, 2)
            rows = ef[:, 0, :].rearrange("p (h e) -> p h e", h=GR)
            least, base, top, span = (SG[0:NR, i] for i in range(4))
            link(dve.tensor_reduce(least, rows, AX.X, ALU.min))
            link(dve.tensor_reduce(top, rows, AX.X, ALU.max))
            R = 1.5 * 2.0 ** 23
            link(dve.tensor_scalar(base, least, 0.5, -0.25, ALU.mult, ALU.add))
            link(dve.tensor_scalar(base, base, R, -R, ALU.add, ALU.add))
            link(dve.tensor_scalar(base, base, 2.0, float(NPAD - WIN), ALU.mult, ALU.min))
            link(dve.tensor_tensor(span, top, base, ALU.subtract))
            dve.wait_ge(consts_ready, 2)
            for h in range(GR):
                dve.tensor_scalar(eb[:, h * NR:(h + 1) * NR], ident[0:NR, 0:NR], base[:, h:h + 1], None, ALU.mult)
            dve.tensor_scalar(eb[:, GR * NR:GR * NR + GR], span, float(WIN), None, ALU.is_ge)
            dve.tensor_tensor(eb[:, GR * NR + GR:NF], top, least, ALU.is_equal).then_inc(edges_diag, 1)

            dve.wait_ge(edges_turned, 2)
            lov, hiv, dv = lo[0:TP], hi[0:TP], dcol[0:TP]
            srcp = ps[0:TP, 7, 0:GR * CK * NR].rearrange("p (k g) -> p k g", k=GR * CK)
            dstp = ps[0:TP, 6, 0:GR * CK * NR].rearrange("p (k g) -> p k g", k=GR * CK)
            dve.tensor_copy(dv, dstp)
            link(dve.tensor_scalar(lov, srcp, 1.0 / TP, 0.5 / TP - 0.5, ALU.mult, ALU.add))
            link(dve.tensor_scalar(hiv, lov, R, -R, ALU.add, ALU.add))
            dve.scalar_tensor_tensor(lov, hiv, -float(TP), srcp, ALU.mult, ALU.add)
            link(dve.tensor_scalar(hiv, hiv, float(WIN), 1.0, ALU.mult, ALU.add))
            dve.wait_ge(edges_spread, 1)
            flags = ps[:, 5, GR * NR:NF].rearrange("p (a h) -> p a h", a=2)
            link(dve.tensor_reduce(fl[:, 0:2], flags, AX.X, ALU.add))
            dve.tensor_scalar(fl[:, 2:3], fl[:, 0:1], 1.0, None, ALU.is_lt)
            link(dve.tensor_scalar(fl[:, 3:4], fl[:, 1:2], float(SAME), None, ALU.is_lt))
            link(dve.tensor_tensor(fl[:, 4:5], fl[:, 2:3], fl[:, 3:4], ALU.mult))
            dve.tensor_scalar(nwin_i[0:1, 0:1], fl[0:1, 4:5], -float(NWIN - 1), float(NWIN), ALU.mult, ALU.add)
            link(dve.tensor_scalar(basebc[:].rearrange("p h g -> p (h g)"), ps[:, 5, 0:GR * NR], fl[:, 4:5], None,
                                   ALU.mult))
            dve.tensor_scalar(base_i[:].rearrange("p (g h) -> p h g", h=GR), basebc[0:1], 0.5, None,
                              ALU.mult).then_inc(table_ready, 1)

            def find_q(step):
                bb = basebc[0:TP].rearrange("p h (c g) -> p h c g", c=1).to_broadcast([TP, GR, CK, NR])
                qv = q[0:TP]
                step(dve.tensor_tensor(qv.rearrange("p (h c) g -> p h c g", h=GR),
                                       dv.rearrange("p (h c) g -> p h c g", h=GR), bb, ALU.subtract))
                step(dve.tensor_scalar(tmp, qv, 0.0, None, ALU.is_ge))
                step(dve.scalar_tensor_tensor(tmp, qv, float(WIN), tmp, ALU.is_lt, ALU.mult))
                step(dve.tensor_tensor(qv, qv, hiv, ALU.add))
                step(dve.tensor_tensor(qv, qv, tmp, ALU.mult))
                step(dve.tensor_scalar(qv, qv, -1.0, None, ALU.add))

            tmp = inside[0:TP]
            find_q(link)

            def onehots(s, r, row):
                if not (isinstance(s, int) and s < RING):
                    dve.wait_ge(counts_ready, s - RING + 1)
                for k in range(CK):
                    b = (r % GR) * CK + k
                    dve.tensor_scalar(lohot[0:TP, r, k, :], iota_lo[0:TP, :], lo[0:TP, b, bass.ds(row, 1)],
                                      None, ALU.is_equal)
                    ins = dve.tensor_scalar(qhot[0:TP, r, k, :], iota_q[0:TP, :], q[0:TP, b, bass.ds(row, 1)],
                                            None, ALU.is_equal)
                ins.then_inc(onehots_made, 1)

            def pow2(name, source):
                link(dve.tensor_scalar(c("t_" + name), source, 2.0 ** -40, None, ALU.max))
                link(dve.tensor_scalar(c("p_" + name).bitcast(I32), c("t_" + name).bitcast(I32), 0x7F800000, None,
                                       ALU.bitwise_and))
                link(dve.reciprocal(c("r_" + name), c("p_" + name)))

            def scale(name):
                n = ORDER.index(name)
                dve.wait_ge(max_spread, n + 1)
                pow2(name, c("all" + name))
                ins = dve.tensor_scalar(c("s_" + name), c("r_" + name), 8192.0, None, ALU.mult)
                own[0] += 1
                ins.then_inc(dve_step, 1)
                dve.wait_ge(dve_step, own[0])

            def signal(s):
                dve.sem_inc(s, 1)

            def tensor_max(name, n, cols):
                dve.tensor_reduce(c("max" + name), mx[:, cols:cols + n], AX.X, ALU.max).then_inc(maxes_ready, 1)

            def wmax(name, k):
                dve.wait_ge(w_in[name], 16 * KT // 2)
                dve.tensor_reduce(mx[:, bass.ds(MC[name] + k // 2, 1)],
                                  WN[name][1][:, bass.ds(k + 1, 2)].rearrange("p k h d -> p (k h d)").bitcast(F32),
                                  AX.X, ALU.max, apply_absolute_value=True).then_inc(max_done, 1)

            def lsplit(name, k):
                n = SPLIT.index(name)
                dve.wait_ge(w_high, n * KT + k + 1)
                w, wr, _ = WN[name]
                dve.scalar_tensor_tensor(w[:, bass.ds(k, 1), 1, :].rearrange("p k d -> p (k d)"),
                                         wr[:, bass.ds(k + 1, 1)].rearrange("p k h d -> p (k h d)").bitcast(F32),
                                         c("s_" + name),
                                         w[:, bass.ds(k, 1), 0, :].rearrange("p k d -> p (k d)"),
                                         ALU.mult, ALU.subtract).then_inc(w_low, 1)

            def xlow(j):
                dve.wait_ge(high_ready, j + 1)
                dve.scalar_tensor_tensor(xT[1][:, :, j * TP:(j + 1) * TP],
                                         bank(2 * (j % 3)).rearrange("p (k n) -> p k n", n=P)[:, :, 0:TP],
                                         c("s_x"), xT[0][:, :, j * TP:(j + 1) * TP],
                                         ALU.mult, ALU.subtract).then_inc(panel_out, 1)

            for s in range(12):
                onehots(s, s % RING, s // GR)
            dve.wait_ge(sums_done, JT)
            tensor_max("x", JT, 0)
            for s in range(12, EARLY):
                onehots(s, s % RING, s // GR)
            scale("x")
            signal(scale_ready)
            for n in range(KT // 2):
                xlow(2 * n)
                xlow(2 * n + 1)
                dve.wait_ge(wn0_in[n], 16)
                dve.tensor_reduce(mx[:, MC["wn0"] + 2 * n:MC["wn0"] + 2 * n + 1],
                                  raw(ws, 2 * n).rearrange("p k d -> p (k d)"),
                                  AX.X, ALU.max, apply_absolute_value=True).then_inc(max_done, 1)
            for j in range(KT, JT):
                xlow(j)
            dve.wait_ge(max_done, KT // 2)
            dve.wait_ge(sums_done, JT + KT // 2)
            tensor_max("wn0", KT, MC["wn0"])
            dve.wait_ge(b0_in, 16)
            dve.tensor_reduce(c("maxb0"), b0c[:], AX.X, ALU.max, apply_absolute_value=True).then_inc(maxes_ready, 1)
            scale("wn0")
            signal(scale_ready)
            for k in range(KT):
                lsplit("wn0", k)

            def low(t, r, layer):
                dve.wait_ge(high_ready, (1 + layer) * JT + t + 1)
                p = bank(2 * r)[0:TP]
                if layer == 0:
                    dve.scalar_tensor_tensor(zh[0:TP, 1:KT + 1, 1, bass.ds(t * P, P)],
                                             p.rearrange("p (f c) -> p f c", f=KT), 2.0 ** -13,
                                             zh[0:TP, 1:KT + 1, 0, bass.ds(t * P, P)],
                                             ALU.mult, ALU.subtract).then_inc(panel_out, 1)
                else:
                    dve.scalar_tensor_tensor(z1[1][:, bass.ds(t, 1), :].rearrange("p j d -> p (j d)"), p,
                                             c("s_z1", TP), z1[0][:, bass.ds(t, 1), :].rearrange("p j d -> p (j d)"),
                                             ALU.mult, ALU.subtract).then_inc(panel_out, 1)

            def groups(i, extra, layer=0):
                for r in range(2):
                    t = 2 * i + r
                    for g in range(GT):
                        if layer == 0 and not (isinstance(t, int) and t == JT - 1):
                            onehots(EARLY + t * GT + g, g % RING, (EARLY + t * GT) // GR + g // GR
                                    if isinstance(t, int) else EARLY // GR + t * (GT // GR) + g // GR)
                        if g == (2 if layer == 0 else 0) and not (isinstance(i, int) and t == 0):
                            low(t - 1, 1 - r, layer)
                        if g in (6, 12):
                            extra(i, 2 * r + g // 6 - 1)

            def nothing(i, m):
                pass

            groups(0, nothing)
            groups(1, nothing)
            dve.wait_ge(sums_done, JT + KT // 2 + KT)
            tensor_max("ws0", KT, MC["ws0"])
            scale("ws0")
            signal(scale_ready)
            with dve.Fori(2, 4) as i:
                groups(i, lambda i, m: lsplit("ws0", 4 * i - 8 + m))
            groups(4, nothing)

            nwin = dve.value_load(nwin_i[0:1, 0:1], min_val=1, max_val=NWIN)
            with dve.If(nwin > 1):
                with dve.Fori(1, nwin) as w:
                    dve.wait_ge(onehots_made, w * NG)
                    n_step = [0]

                    def step(ins):
                        n_step[0] += 1
                        ins.then_inc(win_step, 1)
                        dve.wait_ge(win_step, (w - 1) * 7 + n_step[0])

                    step(dve.tensor_scalar(basebc[:], basebc[:], float(WIN), None, ALU.add))
                    find_q(step)
                    apart(dve)
                    with dve.Fori(0, NG // RING) as i:
                        for r in range(RING):
                            onehots(w * NG + RING * i + r, r, i * (RING // GR) + r // GR)

            def mul(o, a, b, f=1.0):
                link(dve.scalar_tensor_tensor(c(o), c(a), f, c(b), ALU.mult, ALU.mult))

            link(dve.tensor_tensor(c("pw"), c("p_wn0"), c("p_ws0"), ALU.add))
            mul("bound", "p_x", "pw", 4.0)
            dve.wait_ge(max_spread, ORDER.index("b0") + 1)
            link(dve.tensor_tensor(c("bound"), c("bound"), c("allb0"), ALU.add))
            pow2("h", c("bound"))
            link(dve.tensor_scalar(c("s_h"), c("r_h"), 2.0 ** 14, None, ALU.mult))
            mul("cs", "p_x", "p_ws0", 2.0 ** -26)
            mul("cs", "cs", "s_h")
            mul("ca", "p_x", "p_wn0", 2.0 ** -13)
            mul("ca", "ca", "s_h")
            link(dve.tensor_scalar(b0h[:], b0c[:], c("s_h"), None, ALU.mult))
            low(JT - 1, 1, 0)
            dve.wait_ge(counts_added, nwin * NG)
            dve.tensor_copy(AF[0:TP], A[0:TP]).then_inc(A_ready, 1)
            dve.wait_ge(deg_ready, 1)
            link(dve.tensor_scalar(dinvT[0:TP], ps[0:TP, 6, 0:JT], 1.0, None, ALU.max))
            link(dve.reciprocal(dinvT[0:TP], dinvT[0:TP]))
            dve.tensor_tensor(dp, dinvT[0:TP].rearrange("p (j a) -> p j a", a=1).to_broadcast([TP, JT, TP]),
                              ident[0:TP, 0:TP].rearrange("p (a n) -> p a n", a=1).to_broadcast([TP, JT, TP]),
                              ALU.mult).then_inc(dinv_diag, 1)
            for n in range(3):
                m = min(4, JT - 4 * n) * TP
                dve.wait_ge(dinv_spread, n + 1)
                link(dve.tensor_scalar(dinvbc[:, 4 * n * TP:4 * n * TP + m], ps[:, DEG[n], 0:m], c("ca"), None,
                                       ALU.mult))
            signal(dinv_ready)

            def hlow(f, n):
                dve.wait_ge(h_high, 3 * f + n + 1)
                dve.tensor_tensor(zflat[:, bass.ds((2 * f + 1) * BLK + CO[n], CH[n])], h32[:, n, 0:CH[n]],
                                  zflat[:, bass.ds(2 * f * BLK + CO[n], CH[n])], ALU.subtract).then_inc(h_low, 1)
                dve.tensor_reduce(hmx[:, bass.ds(3 * f + n, 1)], h32[:, n, 0:CH[n]], AX.X,
                                  ALU.max).then_inc(hmax_done, 1)

            def unit(f, n):
                v = 3 * f + n
                dve.wait_ge(unit_ready, v + 1)
                dve.tensor_tensor(pre[:, n, 0:CH[n]], ps[:, n, 0:CH[n]], dinvbc[:, CO[n]:CO[n] + CH[n]],
                                  ALU.mult).then_inc(dsum, 1)
                dve.wait_ge(dsum, v + 1)
                dve.scalar_tensor_tensor(pre[:, n, 0:CH[n]], ps[:, SELF[n], 0:CH[n]], c("cs"), pre[:, n, 0:CH[n]],
                                         ALU.mult, ALU.add).then_inc(pre_ready, 1)

            def units(f):
                for n in range(3):
                    unit(f, n)
                    if n:
                        hlow(f, n - 1)
                    elif not (isinstance(f, int) and f == 0):
                        hlow(f - 1, 2)

            units(0)
            with dve.Fori(1, 3) as f:
                units(f)
                for k in range(2):
                    wmax("wn1", 4 * f - 4 + 2 * k)
            dve.wait_ge(max_done, 2 * (KT // 2))
            tensor_max("wn1", KT // 2, MC["wn1"])
            scale("wn1")
            signal(scale_ready)
            with dve.Fori(3, KT - 1) as f:
                units(f)
                for k in range(2):
                    lsplit("wn1", 2 * f - 6 + k)
            units(KT - 1)
            hlow(KT - 1, 2)
            dve.wait_ge(hmax_done, 3 * KT)

            dve.tensor_reduce(c("maxh"), hmx[:], AX.X, ALU.max).then_inc(maxes_ready, 1)
            dve.wait_ge(max_spread, ORDER.index("h") + 1)
            pow2("hs", c("allh"))
            link(dve.tensor_scalar(c("s_z1"), c("r_hs"), 2.0 ** -10, None, ALU.mult))
            signal(scale_ready)
            mul("ca1", "p_h", "p_wn1", 2.0 ** -17)
            mul("ca1", "ca1", "p_hs")
            link(dve.tensor_scalar(dinvT[0:TP], dinvT[0:TP], c("ca1", TP), None, ALU.mult))

            groups(0, nothing, 1)
            groups(1, lambda i, m: wmax("ws1", 2 * m), 1)
            dve.wait_ge(max_done, 3 * (KT // 2))
            tensor_max("ws1", KT // 2, MC["ws1"])
            scale("ws1")
            signal(scale_ready)
            mul("cs1", "p_h", "p_ws1", 2.0 ** -27)
            with dve.Fori(2, 4) as i:
                groups(i, lambda i, m: lsplit("ws1", 4 * i - 8 + m), 1)
            groups(4, nothing, 1)
            low(JT - 1, 1, 1)

            def finish(i, r, first):
                t = 2 * i + r
                g = 4 * (1 - r)
                y = ybuf[r]
                dve.wait_ge(xb_ready, t + 1)
                dve.wait_ge(out_ready, t + 1)
                if not first:
                    dve.wait_ge(o_ready, t - 1)
                dve.scalar_tensor_tensor(y, bank(g + 2)[0:TP], dinvT[0:TP, bass.ds(t, 1)], xres[r],
                                         ALU.mult, ALU.add).then_inc(y_part, 1)
                dve.wait_ge(y_part, t + 1)
                dve.scalar_tensor_tensor(y, bank(g)[0:TP], c("cs1", TP), y, ALU.mult, ALU.add).then_inc(y_ready, 1)
                dve.wait_ge(y_ready, t + 1)
                for h in range(2):
                    ins = dve.bn_stats(st[0:TP, r, 6 * h:6 * h + 6], y[:, h * HD:(h + 1) * HD])
                ins.then_inc(stat_ready, 1)
                dve.wait_ge(stat_ready, t + 1)
                apart(dve)
                dve.bn_aggr(mv[0:TP, r, :], st[0:TP, r, :]).then_inc(aggr_ready, 1)
                dve.wait_ge(aggr_ready, t + 1)
                dve.tensor_scalar(ln[0:TP, r, 0:1], mv[0:TP, r, 1:2], 1e-5, None, ALU.add).then_inc(var_ready, 1)
                dve.wait_ge(std_ready, t + 1)
                dve.reciprocal(ln[0:TP, r, 2:3], ln[0:TP, r, 1:2]).then_inc(rstd_ready, 1)
                dve.wait_ge(rstd_ready, t + 1)
                dve.scalar_tensor_tensor(ln[0:TP, r, 3:4], mv[0:TP, r, 0:1], -1.0, ln[0:TP, r, 2:3],
                                         ALU.mult, ALU.mult).then_inc(shift_ready, 1)

            finish(0, 0, True)
            finish(0, 1, True)
            with dve.Fori(1, IT) as i:
                for r in range(2):
                    finish(i, r, False)


_INS = ["x", "src", "dst", "L0_gnn_W_neigh0", "L0_gnn_W_self0", "L0_gnn_b0", "L0_gnn_W_neigh1", "L0_gnn_W_self1",
        "L0_gnn_b1"]


def kernel(**inputs):
    import numpy as _np
    import concourse.bacc as _bacc
    from concourse import mybir as _mybir
    from concourse.bass_utils import run_bass_kernel_spmd as _run

    nc = _bacc.Bacc("TRN2", target_bir_lowering=False, num_devices=1)
    arrays, args = {}, []
    for name in _INS:
        a = _np.ascontiguousarray(inputs[name])
        arrays[f"in_{name}"] = a
        args.append(nc.dram_tensor(f"in_{name}", a.shape, _mybir.dt.from_np(a.dtype), kind="ExternalInput").ap())
    args.append(nc.dram_tensor("out_0", inputs["x"].shape, _mybir.dt.float32, kind="ExternalOutput").ap())
    gnn_kernel(nc, *args)
    r = _run(nc, [arrays], core_ids=[0])
    return r.results[0]["out_0"]
```

```python
from contextlib import ExitStack

import concourse.bass as bass
from concourse import mybir

ALU = mybir.AluOpType
ACT = mybir.ActivationFunctionType
AX = mybir.AxisListType
F32 = mybir.dt.float32
F16 = mybir.dt.float16
I32 = mybir.dt.int32
U16 = mybir.dt.uint16
RMAX = bass.bass_isa.ReduceOp.max

P = 128
WIN = 24
CK = 2
GR = 2
RING = 4
HOT = 8
LOT = 8


def gnn_kernel(nc, x, src, dst, Wn0, Ws0, b0, Wn1, Ws1, b1, out):
    N, D = x.shape
    E = src.shape[0]
    TP = 125
    JT = N // TP
    KT = D // P
    HD = D // 2
    GE = CK * TP
    NG = E // GE
    NWIN = -(-N // WIN)
    NPAD = NWIN * WIN
    HN = JT * WIN
    assert N == TP * JT and D == P * KT and E == GE * NG and HD <= 512 and HN <= 512
    CH = [420, 420, N - 840]
    CO = [0, 420, 840]
    DEG = (6, 7, 2)
    SELF = (4, 5, 3)
    BLK = JT * P
    RE = GR * GE
    NR = NG // GR
    GT = NG // JT
    EARLY = HOT
    LATE = NG - EARLY - (JT - 1) * GT
    GK = GT // KT
    IT = JT // 2
    SAME = 7
    assert GT == GK * KT and GT % HOT == 0 and GT == 2 * LOT and LATE % HOT == 0 and 0 < LATE <= GT and NR * RE == E
    assert SAME * GE + 2 * (GE - 1) <= 2048 + GE

    with ExitStack() as ctx:
        def sb(name, shape, dt):
            return ctx.enter_context(nc.sbuf_tensor(name, shape, dt))

        def sem(name):
            return ctx.enter_context(nc.semaphore(name))

        xz = sb("xz", [P, 2 * JT * D], F16)
        zh = sb("zh", [P, KT + 1, 2, BLK], F16)
        wn = sb("wn", [P, KT + 1, 2, D], F16)
        ws = sb("ws", [P, KT + 1, 2, D], F16)
        A = sb("A", [P, JT, NPAD], U16)
        scratch = sb("scratch", [P, 5120], F16)
        lohot = sb("lohot", [P, HOT, CK, P], F16)
        table = sb("table", [P, 5, GR * CK, NR], F32)
        basebc = sb("basebc", [P, NG], F32)
        base_i = sb("base_i", [1, NG], I32)
        iota_lo = sb("iota_lo", [P, P], F16)
        iota_q = sb("iota_q", [P, HN], F16)
        ident = sb("ident", [P, P], F32)
        ones = sb("ones", [P, P], F32)
        ones16 = sb("ones16", [P, P], F16)
        dinvT = sb("dinvT", [P, JT], F32)
        b0c = sb("b0c", [P, KT], F32)
        b0h = sb("b0h", [P, KT], F32)
        mx = sb("mx", [P, 5 * KT + 16], F32)
        hmx = sb("hmx", [P, 3 * KT], F32)
        S = sb("S", [P, 64], F32)
        nwin_i = sb("nwin_i", [1, 2], I32)
        SG = sb("SG", [P, 2, GR], F32)
        fl = sb("fl", [P, 8], F32)
        st = sb("st", [P, 2, 12], F32)
        mv = sb("mv", [P, 2, 2], F32)
        ln = sb("ln", [P, 2, 4], F32)
        ps = ctx.enter_context(nc.psum_tensor("ps", [P, 8, 512], F32))

        xT = [xz[:, i * KT * N:(i + 1) * KT * N].rearrange("p (k n) -> p k n", k=KT) for i in range(2)]
        z1 = [xz[0:TP, i * JT * D:(i + 1) * JT * D].rearrange("p (j d) -> p j d", j=JT) for i in range(2)]
        zflat = zh[:].rearrange("p k h n -> p (k h n)")
        xraw = zflat[:, 0:2 * JT * D].bitcast(F32).rearrange("p (j d) -> p j d", j=JT)
        lo, q, hi, dcol, inside = (table[:, i] for i in range(5))
        dinvbc = table[:].rearrange("p a k g -> p (a k g)")[:, 0:N]
        AF = A[:].bitcast(F16)
        A32 = A[:].bitcast(I32)
        QH = HOT * CK * HN
        qhot = scratch[:, 0:QH].rearrange("p (s c n) -> p s c n", s=HOT, c=CK)
        stage = scratch[:, QH:QH + RING * HN].bitcast(U16).rearrange("p (s j w) -> p s j w", s=RING, j=JT)
        stage32 = scratch[:, QH:QH + RING * HN].bitcast(I32).rearrange("p (s j w) -> p s j w", s=RING, j=JT)
        pre = scratch[:, 0:2 * 3 * 420].bitcast(F32).rearrange("p (n c) -> p n c", n=3)
        h32 = scratch[:, 2 * 3 * 420:4 * 3 * 420].bitcast(F32).rearrange("p (n c) -> p n c", n=3)
        dp = scratch[0:TP, 0:2 * N].bitcast(F32).rearrange("p (j n) -> p j n", j=JT)
        eraw = xz[0:NR, 0:4 * RE].bitcast(I32).rearrange("p (t e) -> p t e", t=2)
        ef = xz[0:NR, 4 * RE:8 * RE].bitcast(F32).rearrange("p (t e) -> p t e", t=2)
        eb = xz[0:NR, 8 * RE:8 * RE + 4 * NG].bitcast(F32).rearrange("p (a g h) -> p a g h", a=2, h=GR)
        lt = xz[:, 8 * RE + 4 * NG:8 * RE + 10 * NG].bitcast(F32).rearrange("p (a g) -> p a g", a=3)
        gflag = lt[:, 2]
        unread = xz[:, 16 * D:17 * D]
        wnf = wn[:].rearrange("p k h d -> p k (h d)").bitcast(F32)
        b1bc = wnf[0:TP, 0, :]
        xres = [wnf[0:TP, 1 + i, :] for i in range(2)]
        ybuf = [wnf[0:TP, 3 + i, :] for i in range(2)]
        obuf = [wnf[0:TP, 5 + i, :] for i in range(2)]

        def raw(w, k, n=1):
            return w[:, k + 1:k + 1 + n].rearrange("p k h d -> p k (h d)").bitcast(F32)

        rounded = scratch[0:TP, 0:NPAD]
        left = scratch[0:TP, NPAD:2 * NPAD]
        rest = nc.dram_tensor("rest", [TP, JT, NPAD], F16).ap()
        slices = lohot[0:TP].rearrange("p s c n -> p (s c n)")[:, 0:2 * CH[0]].rearrange("p (i n) -> p i n", i=2)

        def bank(b, n=2):
            return ps[:, b:b + n, :].rearrange("p b c -> p (b c)")

        col = {}

        def c(name, rows=P):
            i = col.setdefault(name, len(col))
            assert i < 64, name
            return S[0:rows, i:i + 1]

        edges_in = sem("edges_in")
        x_in = [sem(f"x_in{j}") for j in range(JT)]
        wn0_in = [sem(f"wn0_in{k}") for k in range(KT // 2)]
        w_in = {n: sem(f"{n}_in") for n in ("ws0", "wn1", "ws1")}
        b0_in = sem("b0_in")
        b1_in = sem("b1_in")
        consts_ready = sem("consts_ready")
        A_zeroed = sem("A_zeroed")
        ws0_scaled = sem("ws0_scaled")
        dve_step = sem("dve_step")
        pool_step = sem("pool_step")
        edges_float = sem("edges_float")
        edges_turned = sem("edges_turned")
        edges_diag = sem("edges_diag")
        edges_spread = sem("edges_spread")
        table_ready = sem("table_ready")
        onehots_made = sem("onehots_made")
        counts_ready = sem("counts_ready")
        counts_copied = sem("counts_copied")
        counts_added = sem("counts_added")
        passed = sem("passed")
        sums_done = sem("sums_done")
        win_step = sem("win_step")
        max_done = sem("max_done")
        maxes_ready = sem("maxes_ready")
        max_spread = sem("max_spread")
        scale_ready = sem("scale_ready")
        panel_ready = sem("panel_ready")
        high_ready = sem("high_ready")
        panel_out = sem("panel_out")
        w_high = sem("w_high")
        w_low = sem("w_low")
        A_ready = sem("A_ready")
        deg_ready = sem("deg_ready")
        deg_read = sem("deg_read")
        unit_ready = sem("unit_ready")
        pre_ready = sem("pre_ready")
        dsum = sem("dsum")
        h32_ready = sem("h32_ready")
        h_high = sem("h_high")
        h_low = sem("h_low")
        hmax_done = sem("hmax_done")
        self_ready = sem("self_ready")
        out_ready = sem("out_ready")
        x_again = [sem(f"x_again{i}") for i in range(2)]
        xb_ready = sem("xb_ready")
        y_part = sem("y_part")
        y_ready = sem("y_ready")
        stat_ready = sem("stat_ready")
        aggr_ready = sem("aggr_ready")
        var_ready = sem("var_ready")
        std_ready = sem("std_ready")
        rstd_ready = sem("rstd_ready")
        shift_ready = sem("shift_ready")
        o_ready = [sem(f"o_ready{h}") for h in range(2)]
        o_stored = [sem(f"o_stored{i}") for i in range(2)]
        rest_made = sem("rest_made")
        rest_step = sem("rest_step")
        rest_stored = sem("rest_stored")
        rest_in = [sem(f"rest_in{i}") for i in range(2)]
        rest_used = sem("rest_used")

        block = ctx.enter_context(nc.Block())

        WN = {"wn0": (wn, ws, Wn0), "ws0": (ws, ws, Ws0), "wn1": (wn, wn, Wn1), "ws1": (ws, ws, Ws1)}
        ORDER = ["x", "b0", "wn0", "ws0", "wn1", "h", "ws1"]
        SPLIT = ["wn0", "ws0", "wn1", "ws1"]

        MC = {"x": 0} | {n: JT + KT * m for m, n in enumerate(SPLIT)}

        def load_weights(eng, name):
            _, buf, dram = WN[name]
            d = dram.rearrange("(k p) d -> p k d", p=P)
            for k in range(0, KT, 2):
                landed = wn0_in[k // 2] if name == "wn0" else w_in[name]
                eng.dma_start(raw(buf, k, 2), d[:, k:k + 2, :]).then_inc(landed, 16)

        def low_part(eng, name, k):
            n = SPLIT.index(name)
            eng.wait_ge(w_high, n * KT + k + 1)
            w, wr, _ = WN[name]
            eng.scalar_tensor_tensor(w[:, bass.ds(k, 1), 1, :].rearrange("p k d -> p (k d)"),
                                     wr[:, bass.ds(k + 1, 1)].rearrange("p k h d -> p (k h d)").bitcast(F32),
                                     c("s_" + name),
                                     w[:, bass.ds(k, 1), 0, :].rearrange("p k d -> p (k d)"),
                                     ALU.mult, ALU.subtract).then_inc(w_low, 1)

        UNITS, TILES = 3, 3 + 3 * KT

        def load_slices(eng, turn, start, width):
            for j in range(JT):
                if not (isinstance(turn, int) and turn == 0 and j < 2):
                    eng.wait_ge(rest_used, JT * turn + j - 1)
                eng.dma_start(slices[:, j % 2, 0:width], rest[:, j, bass.ds(start, width)]).then_inc(rest_in[j % 2], 16)

        def slice_in(eng, turn, j):
            eng.wait_ge(rest_in[j % 2], 16 * (turn * (JT // 2) + j // 2 + 1))
            return slices[:, j % 2]

        def apart(eng):
            eng.sem_inc(passed, 1)

        @block.sync
        def _(sp):
            sp.dma_start(eraw[:, 0, :], dst.rearrange("(g e) -> g e", e=RE)).then_inc(edges_in, 16)
            sp.dma_start(eraw[:, 1, :], src.rearrange("(g e) -> g e", e=RE)).then_inc(edges_in, 16)
            for j in range(JT):
                sp.dma_start(xraw[0:TP, j, :], x[j * TP:(j + 1) * TP, :]).then_inc(x_in[j], 16)
            load_weights(sp, "wn0")
            sp.dma_start(b0c[:], b0.rearrange("(f p) -> p f", p=P), allow_slow_non_contiguous=True).then_inc(b0_in, 16)
            sp.wait_ge(w_low, KT)
            load_weights(sp, "ws0")
            sp.wait_ge(panel_ready, 2 * JT)
            load_weights(sp, "wn1")
            sp.wait_ge(table_ready, 1)
            nwin = sp.value_load(nwin_i[0:1, 0:1], min_val=1, max_val=NWIN)
            with sp.If(nwin > 1):
                for j in range(JT):
                    sp.wait_ge(rest_made, j + 1)
                    sp.dma_start(rest[:, j, :], left).then_inc(rest_stored, 16)
                sp.wait_ge(rest_stored, 16 * JT)
                for n in range(3):
                    load_slices(sp, n, CO[n], CH[n])
                with sp.Fori(0, KT) as f:
                    for n in range(3):
                        load_slices(sp, UNITS + 3 * f + n, CO[n], CH[n])
            sp.wait_ge(unit_ready, 3 * KT)
            load_weights(sp, "ws1")
            sp.wait_ge(panel_ready, 3 * JT)
            sp.dma_start(b1bc, b1.rearrange("(a d) -> a d", a=1).to_broadcast([TP, D])).then_inc(b1_in, 16)

            def load_row(i, r, first=False):
                if not first:
                    sp.wait_ge(y_part, 2 * i + r - 1)
                sp.dma_start(xres[r], x[bass.ds((2 * i + r) * TP, TP), :]).then_inc(x_again[r], 16)

            def store_row(i, r):
                for h in (1, 0):
                    half = slice(h * HD, (h + 1) * HD)
                    sp.wait_ge(o_ready[h], 2 * i + r + 1)
                    apart(sp)
                    sp.dma_start(out[bass.ds((2 * i + r) * TP, TP), half], obuf[r][:, half]).then_inc(o_stored[r], 16)

            def tile_slices(t):
                with sp.If(nwin > 1):
                    load_slices(sp, TILES + t, t * TP, TP)

            for r in range(2):
                load_row(0, r, True)
            for r in range(2):
                tile_slices(r)
            with sp.Fori(0, IT - 1) as i:
                for r in range(2):
                    load_row(i + 1, r)
                    store_row(i, r)
                    tile_slices(2 * i + 2 + r)
            for r in range(2):
                store_row(IT - 1, r)
            for r in range(2):
                sp.wait_ge(o_stored[r], 32 * IT)

        @block.gpsimd
        def _(pool):
            own = [0]

            def link(ins):
                own[0] += 1
                ins.then_inc(pool_step, 1)
                pool.wait_ge(pool_step, own[0])

            link(pool.memset(ones[:], 1.0))
            link(pool.memset(ones16[:], 1.0))
            link(pool.affine_select(out=ident[:], in_=ones[:], compare_op=ALU.is_equal, fill=0.0, base=0,
                                    pattern=[[-1, P]], channel_multiplier=1))
            link(pool.memset(mx[:], 0.0))
            pool.iota(iota_lo[:], [[1, P]], base=0, channel_multiplier=0,
                      allow_small_or_imprecise_dtypes=True).then_inc(consts_ready, 1)
            pool.iota(iota_q[:], [[1, HN]], base=0, channel_multiplier=0,
                      allow_small_or_imprecise_dtypes=True).then_inc(consts_ready, 1)
            pool.memset(A32, 0).then_inc(A_zeroed, 1)
            pool.wait_ge(table_ready, 1)
            nwin = pool.value_load(nwin_i[0:1, 0:1], min_val=1, max_val=NWIN)

            def add(s, r, first, base):
                if not first:
                    pool.wait_ge(counts_added, s)
                pool.wait_ge(counts_copied, s + 1)
                apart(pool)
                a = A32[0:TP, :, bass.ds(base, WIN // 2)]
                pool.tensor_tensor(a, a, stage32[0:TP, r], ALU.add).then_inc(counts_added, 1)

            def adds(i):
                _, bases = nc.values_load_multi_w_load_instructions(
                    base_i[0:1, bass.ds(LOT * i, LOT)], engines=[pool.engine], min_val=0,
                    max_val=(NPAD - WIN) // 2, skip_runtime_bounds_check_because="clamped where it is computed")
                for r in range(LOT):
                    add(LOT * i + r, r % RING, isinstance(i, int) and i == 0 and r == 0, bases[r])

            def low_ws0(k, step):
                v = ws[:, bass.ds(k + 1, 1)].rearrange("p k h d -> p (k h d)").bitcast(F32)
                if step == 0:
                    pool.wait_ge(w_high, KT + k + 1)
                    pool.tensor_tensor(v, v, c("s_ws0").to_broadcast([P, 1, D]), ALU.mult).then_inc(ws0_scaled, 1)
                else:
                    pool.wait_ge(ws0_scaled, k + 1)
                    pool.tensor_tensor(ws[:, bass.ds(k, 1), 1, :].rearrange("p k d -> p (k d)"), v,
                                       ws[:, bass.ds(k, 1), 0, :].rearrange("p k d -> p (k d)"),
                                       ALU.subtract).then_inc(w_low, 1)

            def spread(n):
                pool.wait_ge(maxes_ready, n + 1)
                pool.partition_all_reduce(c("all" + ORDER[n]), c("max" + ORDER[n]), P, RMAX).then_inc(max_spread, 1)

            spread(0)
            pool.wait_ge(A_zeroed, 1)
            for i in range(EARLY // LOT):
                adds(i)
            spread(1)
            spread(2)
            with pool.Fori(EARLY // LOT, (EARLY + 3 * GT + GT // 2) // LOT) as i:
                adds(i)
            spread(3)
            for i in range((EARLY + 3 * GT + GT // 2) // LOT, (EARLY + 4 * GT) // LOT):
                adds(i)
            pool.wait_ge(scale_ready, 3)
            with pool.Fori(4, JT - 3) as t:
                for m in range(2):
                    adds(EARLY // LOT + t * (GT // LOT) + m)
                    low_ws0(t - 4, m)
            with pool.Fori(EARLY // LOT + (JT - 3) * (GT // LOT), NG // LOT) as i:
                adds(i)
            with pool.If(nwin > 1):
                with pool.Fori(1, nwin) as w:
                    with pool.Fori(0, NG // RING) as i:
                        for r in range(RING):
                            add(w * NG + RING * i + r, r, False, w * (WIN // 2))
            for n in range(4, 7):
                spread(n)
            pool.wait_ge(b1_in, 16)

            def residual(i):
                for r in range(2):
                    pool.wait_ge(x_again[r], 16 * (i + 1))
                    pool.tensor_tensor(xres[r], xres[r], b1bc, ALU.add).then_inc(xb_ready, 1)

            with pool.Fori(0, IT) as i:
                residual(i)

        @block.tensor
        def _(pe):
            pe.wait_ge(consts_ready, 2)
            for t in range(2):
                pe.wait_ge(edges_float, t + 1)
                for b in range(GR * CK):
                    ins = pe.transpose(ps[0:TP, 6 + t, b * NR:(b + 1) * NR], ef[:, t, b * TP:(b + 1) * TP],
                                       ident[0:NR, 0:NR])
                ins.then_inc(edges_turned, 1)
            pe.wait_ge(edges_diag, 1)
            pe.matmul(ps[:, 5, 0:2 * NG], ones[0:NR, :], eb.rearrange("p a g h -> p (a g h)"), start=True,
                      stop=True).then_inc(edges_spread, 1)

            def count(s, r, slot, banks):
                pe.wait_ge(onehots_made, s + 1)
                if not (isinstance(s, int) and s < banks):
                    pe.wait_ge(counts_copied, s - banks + 1)
                for k in range(CK):
                    ins = pe.matmul(ps[0:TP, 8 - banks + r, 0:HN], lohot[0:TP, slot, k, 0:TP],
                                    qhot[0:TP, slot, k, :],
                                    start=(k == 0), stop=(k == CK - 1))
                ins.then_inc(counts_ready, 1)

            for j in range(JT):
                pe.wait_ge(x_in[j], 16)
                if j == 2:
                    pe.wait_ge(table_ready, 1)
                if j >= 3:
                    pe.wait_ge(panel_out, j - 2)
                for k in range(KT):
                    b, o = divmod(k * P, 512)
                    ins = pe.transpose(ps[:, 2 * (j % 3) + b, o:o + TP], xraw[0:TP, j, k * P:(k + 1) * P],
                                       ident[0:TP, 0:TP])
                ins.then_inc(panel_ready, 1)
                if j == 2:
                    for s in range(EARLY):
                        count(s, s % 2, s % HOT, 2)

            def panel(i, r, lhs, w, layer):
                t = 2 * i + r
                pe.wait_ge(panel_out, (1 + layer) * JT + t - 1)
                if layer == 1 and isinstance(t, int) and t == 1:
                    pe.wait_ge(pre_ready, 3 * KT)
                for k in range(KT):
                    if layer == 0:
                        for g in range(k * GK, (k + 1) * GK):
                            if not (isinstance(t, int) and t == JT - 1 and g >= LATE):
                                count(EARLY + t * GT + g, g % RING, g % HOT, RING)
                        if isinstance(i, int) and t == 0:
                            pe.wait_ge(w_low, k + 1)
                    elif isinstance(i, int) and t == 0:
                        pe.wait_ge(h_low, 3 * (k + 1))
                    for a, bs in ((0, (0, 1)), (1, (0,))):
                        for b in bs:
                            for half in range(2):
                                ins = pe.matmul(ps[0:TP, 2 * r + half, :], lhs(a, k, t),
                                                w[:, k, b, half * HD:(half + 1) * HD],
                                                start=(k == 0 and a == 0 and b == 0),
                                                stop=(k == KT - 1 and a == 1))
                ins.then_inc(panel_ready, 1)

            def node_tiles(lhs, w, layer):
                for r in range(2):
                    panel(0, r, lhs, w, layer)
                with pe.Fori(1, IT - 1 + layer) as i:
                    for r in range(2):
                        panel(i, r, lhs, w, layer)
                if layer == 0:
                    for r in range(2):
                        panel(IT - 1, r, lhs, w, layer)

            pe.wait_ge(table_ready, 1)
            nwin = pe.value_load(nwin_i[0:1, 0:1], min_val=1, max_val=NWIN)
            pe.wait_ge(panel_out, JT)
            node_tiles(lambda a, k, t: xT[a][:, k, bass.ds(t * TP, TP)], wn, 0)
            with pe.If(nwin > 1):
                with pe.Fori(1, nwin) as w:
                    with pe.Fori(0, NG // HOT) as i:
                        for r in range(HOT):
                            count(w * NG + HOT * i + r, r % RING, r, RING)

            def self_part(f, n):
                if not isinstance(f, int):
                    pe.wait_ge(pre_ready, 3 * f + n - 2)
                for k in range(KT):
                    if isinstance(f, int) and n == 0:
                        pe.wait_ge(w_low, KT + k + 1)
                    for a, b in ((0, 0), (0, 1), (1, 0)):
                        pe.matmul(ps[:, SELF[n], 0:CH[n]], ws[:, k, a, bass.ds(f * P, P)],
                                  xT[b][:, k, CO[n]:CO[n] + CH[n]],
                                  start=(k == 0 and a == 0 and b == 0), stop=(k == KT - 1 and a == 1))

            def neighbour_part(f, n, with_rest):
                for j in range(JT):
                    z = [zflat[0:TP, bass.ds((2 * f + 2 + a) * BLK + j * P, P)] for a in range(2)]
                    if with_rest:
                        r = slice_in(pe, UNITS + 3 * f + n, j)
                        for a in range(2):
                            ins = pe.matmul(ps[:, n, 0:CH[n]], z[a], r[:, 0:CH[n]], start=(j == 0 and a == 0),
                                            stop=False)
                        ins.then_inc(rest_used, 1)
                    for a in range(2):
                        ins = pe.matmul(ps[:, n, 0:CH[n]], z[a], AF[0:TP, j, CO[n]:CO[n] + CH[n]],
                                        start=(j == 0 and a == 0 and not with_rest), stop=(j == JT - 1 and a == 1))
                ins.then_inc(unit_ready, 1)

            pe.wait_ge(counts_copied, nwin * NG)
            for n in range(3):
                if n == 2:
                    pe.wait_ge(panel_out, 2 * JT)
                self_part(0, n)

            def neighbours(with_rest):
                for n in range(3):
                    for j in range(JT):
                        if with_rest:
                            r = slice_in(pe, n, j)
                            pe.matmul(ps[:, DEG[n], 0:CH[n]], ones16[0:TP, :], r[:, 0:CH[n]], start=(j == 0),
                                      stop=False).then_inc(rest_used, 1)
                        ins = pe.matmul(ps[:, DEG[n], 0:CH[n]], ones16[0:TP, :], AF[0:TP, j, CO[n]:CO[n] + CH[n]],
                                        start=(j == 0 and not with_rest), stop=(j == JT - 1))
                    ins.then_inc(deg_ready, 1)
                neighbour_part(0, 0, with_rest)
                neighbour_part(0, 1, with_rest)
                pe.wait_ge(deg_read, 3)
                neighbour_part(0, 2, with_rest)
                with pe.Fori(1, KT) as f:
                    for n in range(3):
                        self_part(f, n)
                        neighbour_part(f, n, with_rest)

            pe.wait_ge(A_ready, 1)
            with pe.If(nwin > 1):
                neighbours(True)
            with pe.Else():
                neighbours(False)

            pe.wait_ge(w_low, 3 * KT)
            pe.wait_ge(pre_ready, 3 * KT - 1)
            node_tiles(lambda a, k, t: zh[:, k, a, bass.ds(t * TP, TP)], wn, 1)

            pe.wait_ge(w_low, 4 * KT)

            def tile(i, r, first, with_rest):
                t = 2 * i + r
                g = 4 * (1 - r)
                if not first:
                    pe.wait_ge(y_part, t - 1)
                elif r == 1:
                    pe.wait_ge(panel_out, 3 * JT)
                for k in range(KT):
                    for a, bs in ((0, (0, 1)), (1, (0,))):
                        for b in bs:
                            for half in range(2):
                                ins = pe.matmul(ps[0:TP, g + half, :], zh[:, k, a, bass.ds(t * TP, TP)],
                                                ws[:, k, b, half * HD:(half + 1) * HD],
                                                start=(k == 0 and a == 0 and b == 0),
                                                stop=(k == KT - 1 and a == 1))
                ins.then_inc(self_ready, 1)
                if first and r == 0:
                    pe.wait_ge(panel_out, 3 * JT)
                elif not first:
                    pe.wait_ge(y_ready, 2 * t - 2)
                if with_rest:
                    for j in range(JT):
                        w = slice_in(pe, TILES + t, j)
                        for b in range(2):
                            for half in range(2):
                                ins = pe.matmul(ps[0:TP, g + 2 + half, :], w[:, 0:TP],
                                                z1[b][:, j, half * HD:(half + 1) * HD],
                                                start=(j == 0 and b == 0), stop=False)
                        ins.then_inc(rest_used, 1)
                for half in range(2):
                    for j in range(JT):
                        for b in range(2):
                            ins = pe.matmul(ps[0:TP, g + 2 + half, :], AF[0:TP, j, bass.ds(t * TP, TP)],
                                            z1[b][:, j, half * HD:(half + 1) * HD],
                                            start=(j == 0 and b == 0 and not with_rest),
                                            stop=(j == JT - 1 and b == 1))
                    ins.then_inc(out_ready, 1)

            def tiles(with_rest):
                tile(0, 0, True, with_rest)
                tile(0, 1, True, with_rest)
                with pe.Fori(1, IT) as i:
                    for r in range(2):
                        tile(i, r, False, with_rest)

            with pe.If(nwin > 1):
                tiles(True)
            with pe.Else():
                tiles(False)

        @block.scalar
        def _(act):
            def take(s, r, banks):
                act.wait_ge(counts_ready, s + 1)
                if not (isinstance(s, int) and s < RING):
                    act.wait_ge(counts_added, s - RING + 1)
                full = ps[0:TP, 8 - banks + r % banks, 0:HN]
                act.activation(stage[0:TP, r], full.rearrange("p (j w) -> p j w", j=JT),
                               ACT.Copy).then_inc(counts_copied, 1)

            act.wait_ge(consts_ready, 2)
            for j in range(JT):
                act.wait_ge(x_in[j], 16)
                act.activation(unread[0:TP], xraw[0:TP, j, :], ACT.Abs,
                               accum_out=mx[0:TP, j:j + 1]).then_inc(sums_done, 1)
                act.wait_ge(sums_done, j + 1)
            for s in range(4):
                take(s, s % RING, 2)

            act.wait_ge(scale_ready, 1)
            for j in range(JT):
                act.wait_ge(panel_ready, j + 1)
                act.activation(xT[0][:, :, j * TP:(j + 1) * TP],
                               bank(2 * (j % 3)).rearrange("p (k n) -> p k n", n=P)[:, :, 0:TP],
                               ACT.Copy, scale=c("s_x")).then_inc(high_ready, 1)
                for s in {0: (4, 5), 1: (6,), 2: (7,)}.get(j, ()):
                    take(s, s % RING, 2)
                for k in {1: (0,), 2: (1,), 3: (2,), 4: (3,), 5: (4,), 6: (5, 6), 7: (7,)}.get(j, ()):
                    act.wait_ge(wn0_in[k // 2], 16)
                    act.activation(wn[:, KT, 0, :], raw(ws, k).rearrange("p k d -> p (k d)"), ACT.Abs,
                                   accum_out=mx[:, MC["wn0"] + k:MC["wn0"] + k + 1]).then_inc(sums_done, 1)
                    act.wait_ge(sums_done, JT + k + 1)

            def split(name, k):
                n = SPLIT.index(name)
                if name != "wn0":
                    act.wait_ge(w_low, n * KT + k)
                w, wr, _ = WN[name]
                act.activation(w[:, bass.ds(k, 1), 0, :].rearrange("p k d -> p (k d)"),
                               wr[:, bass.ds(k + 1, 1)].rearrange("p k h d -> p (k h d)").bitcast(F32),
                               ACT.Copy, scale=c("s_" + name)).then_inc(w_high, 1)

            def z0out(a, t):
                return zh[0:TP, 1:KT + 1, a, bass.ds(t * P, P)]

            def row_sums(k):
                act.wait_ge(w_in["ws0"], 16 * KT // 2)
                act.activation(wn[:, KT, 0, :], raw(ws, k).rearrange("p k d -> p (k d)"), ACT.Abs,
                               accum_out=mx[:, MC["ws0"] + k:MC["ws0"] + k + 1]).then_inc(sums_done, 1)
                act.wait_ge(sums_done, JT + KT + k + 1)

            def panels(i, layer, splits=None, sums=False):
                for r in range(2):
                    t = 2 * i + r
                    for g in range(GT):
                        if layer == 0 and isinstance(t, int) and t == 0 and g % GK == 0:
                            for k in range(0 if g == 0 else g // GK + 1, min(g // GK + 2, KT)):
                                split("wn0", k)
                        if layer == 0 and not (isinstance(t, int) and t == JT - 1 and g >= LATE):
                            take(EARLY + t * GT + g, g % RING, RING)
                        if splits == "ws0":
                            if isinstance(t, int) and t == JT - 1:
                                if g in (7, 8, 9):
                                    split(splits, KT - 10 + g)
                            elif g == 6:
                                split(splits, t - 4)
                        elif splits and g in (3, 9):
                            split(splits, 4 * i - 8 + 2 * r + g // 6)
                        if sums and g % 2 and g < (6 if r else 10):
                            row_sums(5 * r + g // 2)
                    act.wait_ge(panel_ready, (1 + layer) * JT + t + 1)
                    p = bank(2 * r)[0:TP]
                    if layer == 0:
                        act.activation(z0out(0, t), p.rearrange("p (f c) -> p f c", f=KT), ACT.Copy,
                                       scale=2.0 ** -13).then_inc(high_ready, 1)
                    else:
                        act.activation(z1[0][:, bass.ds(t, 1), :].rearrange("p j d -> p (j d)"), p, ACT.Copy,
                                       scale=c("s_z1", TP)).then_inc(high_ready, 1)

            act.wait_ge(scale_ready, 2)
            panels(0, 0)
            panels(1, 0, sums=True)
            act.wait_ge(scale_ready, 3)
            with act.Fori(2, 4) as i:
                panels(i, 0, "ws0")
            panels(4, 0, "ws0")
            act.wait_ge(table_ready, 1)
            nwin = act.value_load(nwin_i[0:1, 0:1], min_val=1, max_val=NWIN)
            with act.If(nwin > 1):
                with act.Fori(1, nwin) as w:
                    with act.Fori(0, NG // RING) as i:
                        for r in range(RING):
                            take(w * NG + RING * i + r, r, RING)

            def unit(f, n):
                v = 3 * f + n
                act.wait_ge(pre_ready, v + 1)
                apart(act)
                act.activation(h32[:, n, 0:CH[n]], pre[:, n, 0:CH[n]], ACT.Relu,
                               bias=b0h[:, bass.ds(f, 1)]).then_inc(h32_ready, 1)
                act.wait_ge(h32_ready, v + 1)
                act.activation(zflat[:, bass.ds(2 * f * BLK + CO[n], CH[n])], h32[:, n, 0:CH[n]],
                               ACT.Copy).then_inc(h_high, 1)

            with act.Fori(0, 3) as f:
                for n in range(3):
                    unit(f, n)
            act.wait_ge(scale_ready, 4)
            with act.Fori(3, KT - 1) as f:
                for n in range(3):
                    unit(f, n)
                for k in range(2):
                    split("wn1", 2 * f - 6 + k)
            for n in range(3):
                unit(KT - 1, n)

            act.wait_ge(scale_ready, 5)
            with act.Fori(0, 2) as i:
                panels(i, 1)
            act.wait_ge(scale_ready, 6)
            with act.Fori(2, 4) as i:
                panels(i, 1, "ws1")
            panels(4, 1)

            def finish(i, r, first):
                t = 2 * i + r
                act.wait_ge(var_ready, t + 1)
                act.activation(ln[0:TP, r, 1:2], ln[0:TP, r, 0:1], ACT.Sqrt).then_inc(std_ready, 1)
                act.wait_ge(shift_ready, t + 1)
                if not first:
                    act.wait_ge(o_stored[r], 32 * i)
                act.activation(obuf[r][:, 0:HD], ybuf[r][:, 0:HD], ACT.Identity, bias=ln[0:TP, r, 3:4],
                               scale=ln[0:TP, r, 2:3]).then_inc(o_ready[0], 1)

            finish(0, 0, True)
            finish(0, 1, True)
            with act.Fori(1, IT) as i:
                for r in range(2):
                    finish(i, r, False)

        @block.vector
        def _(dve):
            own = [0]

            def link(ins):
                own[0] += 1
                ins.then_inc(dve_step, 1)
                dve.wait_ge(dve_step, own[0])

            dve.wait_ge(edges_in, 32)
            for t in range(2):
                dve.tensor_copy(ef[:, t, :], eraw[:, t, :]).then_inc(edges_float, 1)
            dve.wait_ge(edges_float, 2)
            rows = ef[:, 0, :].rearrange("p (h e) -> p h e", h=GR)
            least, top = SG[0:NR, 0], SG[0:NR, 1]
            link(dve.tensor_reduce(least, rows, AX.X, ALU.min))
            link(dve.tensor_reduce(top, rows, AX.X, ALU.max))
            dve.wait_ge(consts_ready, 2)
            for m in range(2):
                for h in range(GR):
                    ins = dve.tensor_scalar(eb[:, m, :, h], ident[0:NR, 0:NR], SG[0:NR, m, h:h + 1], None, ALU.mult)
            ins.then_inc(edges_diag, 1)

            dve.wait_ge(edges_turned, 2)
            lov, hiv, dv = lo[0:TP], hi[0:TP], dcol[0:TP]
            srcp = ps[0:TP, 7, 0:GR * CK * NR].rearrange("p (k g) -> p k g", k=GR * CK)
            dstp = ps[0:TP, 6, 0:GR * CK * NR].rearrange("p (k g) -> p k g", k=GR * CK)
            dve.tensor_copy(dv, dstp)
            link(dve.tensor_scalar(lov, srcp, 1.0 / TP, 0.5 / TP - 0.5, ALU.mult, ALU.add))
            R = 1.5 * 2.0 ** 23
            link(dve.tensor_scalar(hiv, lov, R, -R, ALU.add, ALU.add))
            dve.scalar_tensor_tensor(lov, hiv, -float(TP), srcp, ALU.mult, ALU.add)
            link(dve.tensor_scalar(hiv, hiv, float(WIN), 1.0, ALU.mult, ALU.add))
            dve.wait_ge(edges_spread, 1)
            link(dve.tensor_copy(lt[:, 0:2].rearrange("p a g -> p (a g)"), ps[:, 5, 0:2 * NG]))
            least, top = lt[:, 0], lt[:, 1]
            base = basebc[:]
            link(dve.tensor_scalar(base, least, 0.5, -0.25, ALU.mult, ALU.add))
            dve.tensor_tensor(gflag, top, least, ALU.is_equal)
            link(dve.tensor_scalar(base, base, R, -R, ALU.add, ALU.add))
            dve.tensor_reduce(fl[:, 1:2], gflag, AX.X, ALU.add)
            link(dve.tensor_scalar(base, base, 2.0, float(NPAD - WIN), ALU.mult, ALU.min))
            link(dve.tensor_tensor(gflag, top, base, ALU.subtract))
            link(dve.tensor_reduce(fl[:, 0:1], gflag, AX.X, ALU.max))
            link(dve.tensor_tensor(gflag[:, 1:NG], top[:, 0:NG - 1], least[:, 1:NG], ALU.is_gt))
            link(dve.tensor_reduce(fl[:, 2:3], gflag[:, 1:NG], AX.X, ALU.max))
            dve.tensor_scalar(fl[:, 3:4], fl[:, 0:1], float(WIN), None, ALU.is_lt)
            link(dve.tensor_scalar(fl[:, 4:5], fl[:, 1:2], float(SAME), None, ALU.is_lt))
            link(dve.tensor_tensor(fl[:, 5:6], fl[:, 3:4], fl[:, 4:5], ALU.mult))
            link(dve.tensor_tensor(fl[:, 6:7], fl[:, 5:6], fl[:, 2:3], ALU.is_gt))
            dve.tensor_scalar(nwin_i[0:1, 0:1], fl[0:1, 6:7], -float(NWIN - 1), float(NWIN), ALU.mult, ALU.add)
            link(dve.tensor_scalar(base, base, fl[:, 6:7], None, ALU.mult))
            dve.tensor_scalar(base_i[:], basebc[0:1], 0.5, None, ALU.mult).then_inc(table_ready, 1)

            def find_q(step):
                bb = basebc[0:TP].rearrange("p (g h c) -> p h c g", h=GR, c=1).to_broadcast([TP, GR, CK, NR])
                qv = q[0:TP]
                step(dve.tensor_tensor(qv.rearrange("p (h c) g -> p h c g", h=GR),
                                       dv.rearrange("p (h c) g -> p h c g", h=GR), bb, ALU.subtract))
                step(dve.tensor_scalar(tmp, qv, 0.0, None, ALU.is_ge))
                step(dve.scalar_tensor_tensor(tmp, qv, float(WIN), tmp, ALU.is_lt, ALU.mult))
                step(dve.tensor_tensor(qv, qv, hiv, ALU.add))
                step(dve.tensor_tensor(qv, qv, tmp, ALU.mult))
                step(dve.tensor_scalar(qv, qv, -1.0, None, ALU.add))

            tmp = inside[0:TP]
            find_q(link)

            def onehots(s, r, row):
                if not (isinstance(s, int) and s < HOT):
                    dve.wait_ge(counts_ready, s - HOT + 1)
                for k in range(CK):
                    b = (r % GR) * CK + k
                    dve.tensor_scalar(lohot[0:TP, r, k, :], iota_lo[0:TP, :], lo[0:TP, b, bass.ds(row, 1)],
                                      None, ALU.is_equal)
                    ins = dve.tensor_scalar(qhot[0:TP, r, k, :], iota_q[0:TP, :], q[0:TP, b, bass.ds(row, 1)],
                                            None, ALU.is_equal)
                ins.then_inc(onehots_made, 1)

            def pow2(name, source):
                link(dve.tensor_scalar(c("t_" + name), source, 2.0 ** -40, None, ALU.max))
                link(dve.tensor_scalar(c("p_" + name).bitcast(I32), c("t_" + name).bitcast(I32), 0x7F800000, None,
                                       ALU.bitwise_and))
                link(dve.reciprocal(c("r_" + name), c("p_" + name)))

            def scale(name):
                n = ORDER.index(name)
                dve.wait_ge(max_spread, n + 1)
                pow2(name, c("all" + name))
                link(dve.tensor_scalar(c("s_" + name), c("r_" + name), 8192.0, None, ALU.mult))

            def signal(s):
                dve.sem_inc(s, 1)

            def tensor_max(name, n, cols):
                dve.tensor_reduce(c("max" + name), mx[:, cols:cols + n], AX.X, ALU.max).then_inc(maxes_ready, 1)

            def wmax(name, k):
                dve.wait_ge(w_in[name], 16 * KT // 2)
                dve.tensor_reduce(mx[:, bass.ds(MC[name] + k // 2, 1)],
                                  WN[name][1][:, bass.ds(k + 1, 2)].rearrange("p k h d -> p (k h d)").bitcast(F32),
                                  AX.X, ALU.max, apply_absolute_value=True).then_inc(max_done, 1)

            def xlow(j):
                dve.wait_ge(high_ready, j + 1)
                dve.scalar_tensor_tensor(xT[1][:, :, j * TP:(j + 1) * TP],
                                         bank(2 * (j % 3)).rearrange("p (k n) -> p k n", n=P)[:, :, 0:TP],
                                         c("s_x"), xT[0][:, :, j * TP:(j + 1) * TP],
                                         ALU.mult, ALU.subtract).then_inc(panel_out, 1)

            def ahead(s0, n):
                for s in range(s0, s0 + n):
                    onehots(s, s % HOT, s // GR)

            ahead(0, 5)
            dve.wait_ge(sums_done, JT)
            tensor_max("x", JT, 0)
            ahead(5, 1)
            scale("x")
            signal(scale_ready)
            ahead(6, 2)
            for j in range(JT):
                xlow(j)
                if j < HOT - 1:
                    ahead(EARLY + j, 1)
                if j == 7:
                    dve.wait_ge(b0_in, 16)
                    dve.tensor_reduce(c("maxb0"), b0c[:], AX.X, ALU.max,
                                      apply_absolute_value=True).then_inc(maxes_ready, 1)
                    dve.wait_ge(sums_done, JT + KT)
                    tensor_max("wn0", KT, MC["wn0"])
                    ahead(EARLY + j, 1)
                if j == 8:
                    scale("wn0")
                    signal(scale_ready)

            def low(t, r, layer):
                dve.wait_ge(high_ready, (1 + layer) * JT + t + 1)
                p = bank(2 * r)[0:TP]
                if layer == 0:
                    dve.scalar_tensor_tensor(zh[0:TP, 1:KT + 1, 1, bass.ds(t * P, P)],
                                             p.rearrange("p (f c) -> p f c", f=KT), 2.0 ** -13,
                                             zh[0:TP, 1:KT + 1, 0, bass.ds(t * P, P)],
                                             ALU.mult, ALU.subtract).then_inc(panel_out, 1)
                else:
                    dve.scalar_tensor_tensor(z1[1][:, bass.ds(t, 1), :].rearrange("p j d -> p (j d)"), p,
                                             c("s_z1", TP), z1[0][:, bass.ds(t, 1), :].rearrange("p j d -> p (j d)"),
                                             ALU.mult, ALU.subtract).then_inc(panel_out, 1)

            def nothing(i, m):
                pass

            def z_tile(i, r, extra=None):
                t = 2 * i + r
                first = isinstance(t, int) and t == 0
                for g in range(GT):
                    if first and g % GK == 0:
                        low_part(dve, "wn0", g // GK)
                    if not (first and g % 2 or isinstance(t, int) and t == JT - 1 and g >= LATE):
                        n = HOT + g // 2 if first else g
                        onehots(EARLY + t * GT + n, n % HOT, EARLY // GR + t * (GT // GR) + n // GR)
                    if g == 6 and not first:
                        low(t - 1, 1 - r, 0)
                    if extra:
                        extra(g)

            def max_ws0(g):
                if g == GT - 5:
                    dve.wait_ge(sums_done, JT + KT + KT)
                    tensor_max("ws0", KT, MC["ws0"])
                if g == GT - 1:
                    scale("ws0")
                    signal(scale_ready)

            for t in range(4):
                z_tile(t // 2, t % 2, max_ws0 if t == 3 else None)
            with dve.Fori(2, JT // 2 - 1) as i:
                for r in range(2):
                    z_tile(i, r)
            z_tile(JT // 2 - 1, 0, lambda g: low_part(dve, "ws0", {3: 3, 11: 4}[g]) if g in (3, 11) else None)
            z_tile(JT // 2 - 1, 1)
            for k in range(5, KT):
                low_part(dve, "ws0", k)

            def groups(i, extra):
                for r in range(2):
                    if not (isinstance(i, int) and i == 0 and r == 0):
                        low(2 * i + r - 1, 1 - r, 1)
                    for m in range(2):
                        extra(i, 2 * r + m)

            nwin = dve.value_load(nwin_i[0:1, 0:1], min_val=1, max_val=NWIN)
            with dve.If(nwin > 1):
                with dve.Fori(1, nwin) as w:
                    dve.wait_ge(onehots_made, w * NG)
                    n_step = [0]

                    def step(ins):
                        n_step[0] += 1
                        ins.then_inc(win_step, 1)
                        dve.wait_ge(win_step, (w - 1) * 7 + n_step[0])

                    step(dve.tensor_scalar(basebc[:], basebc[:], float(WIN), None, ALU.add))
                    find_q(step)
                    apart(dve)
                    with dve.Fori(0, NG // HOT) as i:
                        for r in range(HOT):
                            onehots(w * NG + HOT * i + r, r, i * (HOT // GR) + r // GR)

            def mul(o, a, b, f=1.0):
                link(dve.scalar_tensor_tensor(c(o), c(a), f, c(b), ALU.mult, ALU.mult))

            link(dve.tensor_tensor(c("pw"), c("p_wn0"), c("p_ws0"), ALU.add))
            mul("bound", "p_x", "pw", 4.0)
            dve.wait_ge(max_spread, ORDER.index("b0") + 1)
            link(dve.tensor_tensor(c("bound"), c("bound"), c("allb0"), ALU.add))
            pow2("h", c("bound"))
            link(dve.tensor_scalar(c("s_h"), c("r_h"), 2.0 ** 14, None, ALU.mult))
            mul("cs", "p_x", "p_ws0", 2.0 ** -26)
            mul("cs", "cs", "s_h")
            mul("ca", "p_x", "p_wn0", 2.0 ** -13)
            mul("ca", "ca", "s_h")
            link(dve.reciprocal(c("r_ca"), c("ca")))
            link(dve.tensor_scalar(b0h[:], b0c[:], c("s_h"), None, ALU.mult))
            low(JT - 1, 1, 0)
            dve.wait_ge(counts_added, nwin * NG)
            apart(dve)
            with dve.If(nwin > 1):
                for j in range(JT):
                    if j:
                        dve.wait_ge(rest_stored, 16 * j)
                    dve.tensor_copy(rounded, A[0:TP, j, :]).then_inc(rest_step, 1)
                    dve.wait_ge(rest_step, j + 1)
                    dve.tensor_tensor(left, A[0:TP, j, :], rounded, ALU.subtract).then_inc(rest_made, 1)
                dve.wait_ge(rest_stored, 16 * JT)
            dve.tensor_copy(AF[0:TP], A[0:TP]).then_inc(A_ready, 1)
            for n in range(3):
                dve.wait_ge(deg_ready, n + 1)
                dve.tensor_scalar(dinvbc[:, CO[n]:CO[n] + CH[n]], ps[:, DEG[n], 0:CH[n]], 1.0, c("r_ca"),
                                  ALU.max, ALU.mult).then_inc(deg_read, 1)
            dve.wait_ge(deg_read, 3)

            def hlow(f, n):
                dve.wait_ge(h_high, 3 * f + n + 1)
                dve.tensor_tensor(zflat[:, bass.ds((2 * f + 1) * BLK + CO[n], CH[n])], h32[:, n, 0:CH[n]],
                                  zflat[:, bass.ds(2 * f * BLK + CO[n], CH[n])], ALU.subtract).then_inc(h_low, 1)
                dve.tensor_reduce(hmx[:, bass.ds(3 * f + n, 1)], h32[:, n, 0:CH[n]], AX.X,
                                  ALU.max).then_inc(hmax_done, 1)

            def unit(f, n):
                v = 3 * f + n
                dve.wait_ge(unit_ready, v + 1)
                dve.tensor_tensor(pre[:, n, 0:CH[n]], ps[:, n, 0:CH[n]], dinvbc[:, CO[n]:CO[n] + CH[n]],
                                  ALU.mult).then_inc(dsum, 1)
                dve.wait_ge(dsum, v + 1)
                dve.scalar_tensor_tensor(pre[:, n, 0:CH[n]], ps[:, SELF[n], 0:CH[n]], c("cs"), pre[:, n, 0:CH[n]],
                                         ALU.mult, ALU.add).then_inc(pre_ready, 1)

            def units(f):
                for n in range(3):
                    if isinstance(f, int) and f == 0:
                        d = dinvbc[:, CO[n]:CO[n] + CH[n]]
                        link(dve.reciprocal(d, d))
                    unit(f, n)
                    if n:
                        hlow(f, n - 1)
                    elif not (isinstance(f, int) and f == 0):
                        hlow(f - 1, 2)

            units(0)
            with dve.Fori(1, 3) as f:
                units(f)
                for k in range(2):
                    wmax("wn1", 4 * f - 4 + 2 * k)
            dve.wait_ge(max_done, KT // 2)
            tensor_max("wn1", KT // 2, MC["wn1"])
            scale("wn1")
            signal(scale_ready)
            with dve.Fori(3, KT - 1) as f:
                units(f)
                for k in range(2):
                    low_part(dve, "wn1", 2 * f - 6 + k)
            units(KT - 1)
            hlow(KT - 1, 2)
            dve.wait_ge(hmax_done, 3 * KT)

            dve.tensor_reduce(c("maxh"), hmx[:], AX.X, ALU.max).then_inc(maxes_ready, 1)
            dve.wait_ge(max_spread, ORDER.index("h") + 1)
            pow2("hs", c("allh"))
            link(dve.tensor_scalar(c("s_z1"), c("r_hs"), 2.0 ** -10, None, ALU.mult))
            signal(scale_ready)
            mul("ca1", "p_h", "p_wn1", 2.0 ** -17)
            mul("ca1", "ca1", "p_hs")
            mul("ca1", "ca1", "r_ca")
            link(dve.tensor_tensor(dp, dinvbc[0:TP].rearrange("p (j n) -> p j n", j=JT),
                                   ident[0:TP, 0:TP].rearrange("p (a n) -> p a n", a=1).to_broadcast([TP, JT, TP]),
                                   ALU.mult))
            link(dve.tensor_reduce(dinvT[0:TP], dp, AX.X, ALU.add))
            link(dve.tensor_scalar(dinvT[0:TP], dinvT[0:TP], c("ca1", TP), None, ALU.mult))

            groups(0, nothing)
            groups(1, lambda i, m: wmax("ws1", 2 * m))
            dve.wait_ge(max_done, 2 * (KT // 2))
            tensor_max("ws1", KT // 2, MC["ws1"])
            scale("ws1")
            signal(scale_ready)
            mul("cs1", "p_h", "p_ws1", 2.0 ** -27)
            with dve.Fori(2, 4) as i:
                groups(i, lambda i, m: low_part(dve, "ws1", 4 * i - 8 + m))
            groups(4, nothing)
            low(JT - 1, 1, 1)

            def finish(i, r, first):
                t = 2 * i + r
                g = 4 * (1 - r)
                y = ybuf[r]
                dve.wait_ge(xb_ready, t + 1)
                dve.wait_ge(self_ready, t + 1)
                if not first:
                    for h in range(2):
                        dve.wait_ge(o_ready[h], t - 1)
                dve.scalar_tensor_tensor(y, bank(g)[0:TP], c("cs1", TP), xres[r], ALU.mult, ALU.add).then_inc(y_part, 1)
                dve.wait_ge(y_part, t + 1)
                for h in range(2):
                    yh = y[:, h * HD:(h + 1) * HD]
                    dve.wait_ge(out_ready, 2 * t + h + 1)
                    apart(dve)
                    dve.scalar_tensor_tensor(yh, ps[0:TP, g + 2 + h, :], dinvT[0:TP, bass.ds(t, 1)], yh,
                                             ALU.mult, ALU.add).then_inc(y_ready, 1)
                    dve.wait_ge(y_ready, 2 * t + h + 1)
                    apart(dve)
                    ins = dve.bn_stats(st[0:TP, r, 6 * h:6 * h + 6], yh)
                ins.then_inc(stat_ready, 1)
                dve.wait_ge(stat_ready, t + 1)
                apart(dve)
                dve.bn_aggr(mv[0:TP, r, :], st[0:TP, r, :]).then_inc(aggr_ready, 1)
                dve.wait_ge(aggr_ready, t + 1)
                dve.tensor_scalar(ln[0:TP, r, 0:1], mv[0:TP, r, 1:2], 1e-5, None, ALU.add).then_inc(var_ready, 1)
                dve.wait_ge(std_ready, t + 1)
                dve.reciprocal(ln[0:TP, r, 2:3], ln[0:TP, r, 1:2]).then_inc(rstd_ready, 1)
                dve.wait_ge(rstd_ready, t + 1)
                dve.scalar_tensor_tensor(ln[0:TP, r, 3:4], mv[0:TP, r, 0:1], -1.0, ln[0:TP, r, 2:3],
                                         ALU.mult, ALU.mult).then_inc(shift_ready, 1)
                dve.wait_ge(shift_ready, t + 1)
                if not first:
                    dve.wait_ge(o_stored[r], 32 * i)
                apart(dve)
                dve.tensor_scalar(obuf[r][:, HD:D], y[:, HD:D], ln[0:TP, r, 2:3], ln[0:TP, r, 3:4],
                                  ALU.mult, ALU.add).then_inc(o_ready[1], 1)

            finish(0, 0, True)
            finish(0, 1, True)
            with dve.Fori(1, IT) as i:
                for r in range(2):
                    finish(i, r, False)


_INS = ["x", "src", "dst", "L0_gnn_W_neigh0", "L0_gnn_W_self0", "L0_gnn_b0", "L0_gnn_W_neigh1", "L0_gnn_W_self1",
        "L0_gnn_b1"]


def kernel(**inputs):
    import numpy as _np
    import concourse.bacc as _bacc
    from concourse import mybir as _mybir
    from concourse.bass_utils import run_bass_kernel_spmd as _run

    nc = _bacc.Bacc("TRN2", target_bir_lowering=False, num_devices=1)
    arrays, args = {}, []
    for name in _INS:
        a = _np.ascontiguousarray(inputs[name])
        arrays[f"in_{name}"] = a
        args.append(nc.dram_tensor(f"in_{name}", a.shape, _mybir.dt.from_np(a.dtype), kind="ExternalInput").ap())
    args.append(nc.dram_tensor("out_0", inputs["x"].shape, _mybir.dt.float32, kind="ExternalOutput").ap())
    gnn_kernel(nc, *args)
    r = _run(nc, [arrays], core_ids=[0])
    return r.results[0]["out_0"]
```
